# Optimizing a Trainium2 kernel written in Bass

```python
import numpy as np
import jax
import jax.numpy as jnp

def _softmax(x, axis=-1):
    return jax.nn.softmax(x, axis=axis)

def _gelu(x):
    return jax.nn.gelu(x, approximate=True)

def _silu(x):
    return jax.nn.silu(x)

def _sigmoid(x):
    return jax.nn.sigmoid(x)

def _layernorm(x, axis=-1, eps=1e-05):
    m = jnp.mean(x, axis=axis, keepdims=True)
    v = jnp.var(x, axis=axis, keepdims=True)
    return (x - m) / jnp.sqrt(v + eps)

def _scatter_add(tgt, idx, src, axis=0):
    return tgt.at[idx].add(src)

def _segment_sum(src, seg, n):
    return jax.ops.segment_sum(src, seg, n)
kernel_name = 'mk_xattn_ffn_d1_seqx_r8_8e2fb5'

def setup_inputs(seed: int=0):
    np.random.seed(seed)
    _w = jnp.asarray

    def _rec_inputs():
        import jax
        import jax.numpy as jnp
        _rk = jax.random.key(seed)
        x = 7.22e-05 + 1 * jax.random.normal(jax.random.fold_in(_rk, 1), (8, 128, 512), jnp.float32)
        _lenS = 128 - jax.random.randint(jax.random.fold_in(_rk, 7), (8,), 0, max(1, 128 // 4) + 1, jnp.int32)
        _lenS2 = 128 - jax.random.randint(jax.random.fold_in(_rk, 8), (8,), 0, max(1, 128 // 4) + 1, jnp.int32)
        _ctx_4096P = jax.random.normal(jax.random.fold_in(_rk, 11), (8, 16, 512), jnp.float32)
        _ctx_4096c = jax.random.dirichlet(jax.random.fold_in(_rk, 511), 0.3 * jnp.ones((16,), jnp.float32), (8, 128))
        _ctx_4096t = jnp.einsum('bsk,bkd->bsd', _ctx_4096c, _ctx_4096P)
        _ctx_4096t = _ctx_4096t * jax.lax.rsqrt(jnp.mean(jnp.square(_ctx_4096t)) + 1e-12) * 0.953939
        ctx_4096 = 4.13588e-05 + 0.999923 * (_ctx_4096t + 0.3 * jax.random.normal(jax.random.fold_in(_rk, 611), (8, 128, 512), jnp.float32))
        _validS = jnp.arange(128)[None, :] < _lenS[:, None]
        _validS2 = jnp.arange(128)[None, :] < _lenS2[:, None]
        _causal = jnp.tril(jnp.ones((128, 128), dtype=bool))
        mask_BxSxS2_bk0 = jnp.logical_not(jnp.broadcast_to(_validS2[:, None, :], (8, 128, 128)))
        return (x, ctx_4096, mask_BxSxS2_bk0)
    x, ctx_4096, mask_BxSxS2_bk0 = _rec_inputs()

    def _L0_xattn_setup():
        import jax, jax.numpy as jnp
        import numpy as np
        B, LQ, LK, D, H, DH = (2, 128, 128, 512, 32, 128)
        EPS = 1e-05

        def _rmsnorm(x, weight):
            var = jnp.mean(jnp.square(x), axis=-1, keepdims=True)
            return x * jax.lax.rsqrt(var + EPS) * weight
        key = jax.random.key(seed)
        ks = jax.random.split(key, 8)
        scale = 0.02
        return {'hidden_states': jax.random.normal(ks[0], (B, LQ, D), jnp.float32), 'key_value_states': jax.random.normal(ks[1], (B, LK, D), jnp.float32), 'attention_mask': jax.random.randint(ks[2], (B, LQ, LK), 0, 2) > 0, 'position_bias': jax.random.normal(ks[3], (H, LQ, LK), jnp.float32), 'ln_weight': jnp.ones((D,), jnp.float32), 'w_q': jax.random.normal(ks[4], (H * DH, D), jnp.float32) * scale, 'w_k': jax.random.normal(ks[5], (H * DH, D), jnp.float32) * scale, 'w_v': jax.random.normal(ks[6], (H * DH, D), jnp.float32) * scale, 'w_out': jax.random.normal(ks[7], (D, H * DH), jnp.float32) * scale}
    _L0_xattn_all = _L0_xattn_setup()
    _L0_xattn_in = {k: v for k, v in _L0_xattn_all.items() if k in ('position_bias', 'ln_weight', 'w_q', 'w_k', 'w_v', 'w_out')}
    del _L0_xattn_all

    def _L0_ffn_setup():
        import jax, jax.numpy as jnp
        import numpy as np
        import math
        E, DK, R = (8, 32, 16)
        SCALING = 16.0 / 16.0
        key = jax.random.key(seed)
        ks = jax.random.split(key, 7)
        Bt, S, Din, Dout = (4, 256, 512, 512)
        x = jax.random.normal(ks[0], (Bt, S, Din), jnp.float32)
        W = jax.random.normal(ks[1], (Dout, Din), jnp.float32) * 0.02
        b = jnp.zeros((Dout,), jnp.float32)
        Wq = jax.random.normal(ks[2], (E * DK, Din), jnp.float32) * 0.02
        Wk = jax.random.normal(ks[3], (E * DK, Din), jnp.float32) * 0.02
        A = jax.random.normal(ks[4], (E, R, Din), jnp.float32) * 0.02
        Bm = jax.random.normal(ks[5], (E, Dout, R), jnp.float32) * 0.02
        return {'x': x, 'W': W, 'b': b, 'Wq': Wq, 'Wk': Wk, 'A': A, 'Bm': Bm}
    _L0_ffn_all = _L0_ffn_setup()
    _L0_ffn_in = {k: v for k, v in _L0_ffn_all.items() if k in ('W', 'b', 'Wq', 'Wk', 'A', 'Bm')}
    del _L0_ffn_all
    return {'x': x, 'ctx_4096': ctx_4096, 'mask_BxSxS2_bk0': mask_BxSxS2_bk0, 'L0_xattn_position_bias': _L0_xattn_in['position_bias'], 'L0_xattn_ln_weight': _L0_xattn_in['ln_weight'], 'L0_xattn_w_q': _L0_xattn_in['w_q'], 'L0_xattn_w_k': _L0_xattn_in['w_k'], 'L0_xattn_w_v': _L0_xattn_in['w_v'], 'L0_xattn_w_out': _L0_xattn_in['w_out'], 'L0_ffn_W': _L0_ffn_in['W'], 'L0_ffn_b': _L0_ffn_in['b'], 'L0_ffn_Wq': _L0_ffn_in['Wq'], 'L0_ffn_Wk': _L0_ffn_in['Wk'], 'L0_ffn_A': _L0_ffn_in['A'], 'L0_ffn_Bm': _L0_ffn_in['Bm']}

def reference(x, ctx_4096, mask_BxSxS2_bk0, L0_xattn_position_bias, L0_xattn_ln_weight, L0_xattn_w_q, L0_xattn_w_k, L0_xattn_w_v, L0_xattn_w_out, L0_ffn_W, L0_ffn_b, L0_ffn_Wq, L0_ffn_Wk, L0_ffn_A, L0_ffn_Bm):
    import jax
    import jax.numpy as jnp

    def _L0_xattn_ref(hidden_states, key_value_states, attention_mask, position_bias, ln_weight, w_q, w_k, w_v, w_out):
        import jax, jax.numpy as jnp
        import numpy as np
        B, LQ, LK, D, H, DH = (2, 128, 128, 512, 32, 128)
        EPS = 1e-05

        def _rmsnorm(x, weight):
            var = jnp.mean(jnp.square(x), axis=-1, keepdims=True)
            return x * jax.lax.rsqrt(var + EPS) * weight
        x = _rmsnorm(hidden_states, ln_weight)
        b, lq, _ = x.shape
        lk = key_value_states.shape[1]
        h_q = (x @ w_q.T).reshape(b, lq, H, DH)
        h_k = (key_value_states @ w_k.T).reshape(b, lk, H, DH)
        h_v = (key_value_states @ w_v.T).reshape(b, lk, H, DH)
        score = jnp.einsum('bqhd,bkhd->bhqk', h_q, h_k)
        score = score + position_bias[None]
        m = attention_mask[:, None]
        score = jnp.where(m, score, -jnp.inf)
        score = jax.nn.softmax(score, axis=-1)
        score = jnp.where(m, score, 0.0)
        attn = jnp.einsum('bhqk,bkhd->bqhd', score, h_v).reshape(b, lq, H * DH)
        out = attn @ w_out.T
        return hidden_states + out

    def _L0_ffn_ref(x, W, b, Wq, Wk, A, Bm):
        import jax, jax.numpy as jnp
        import numpy as np
        import math
        E, DK, R = (8, 32, 16)
        SCALING = 16.0 / 16.0
        Bt, S, Din = x.shape
        result = jnp.einsum('bsi,oi->bso', x, W) + b
        q = jnp.einsum('bsi,ni->bsn', x, Wq).reshape(Bt, S, E, DK)
        k = jnp.einsum('bsi,ni->bsn', x, Wk).reshape(Bt, S, E, DK)
        scores = jnp.einsum('bsed,bsed->bse', q, k) / math.sqrt(DK)
        w = jax.nn.softmax(scores, axis=-1)
        h = jnp.einsum('bsi,eri->bser', x, A)
        combined = jnp.einsum('bse,bser,eor->bso', w, h, Bm) * SCALING
        return result + combined
    x = x + _L0_xattn_ref(_layernorm(x, axis=-1), ctx_4096, mask_BxSxS2_bk0, L0_xattn_position_bias, L0_xattn_ln_weight, L0_xattn_w_q, L0_xattn_w_k, L0_xattn_w_v, L0_xattn_w_out)
    x = x + _L0_ffn_ref(_layernorm(x, axis=-1), L0_ffn_W, L0_ffn_b, L0_ffn_Wq, L0_ffn_Wk, L0_ffn_A, L0_ffn_Bm)
    return x

_drawn_inputs = setup_inputs


def setup_inputs(seed=0):
    import zlib

    import numpy as np

    out = dict(_drawn_inputs(seed))
    spreads = {'L0_xattn_ln_weight': (1.0, 0.2), 'L0_ffn_b': (0.0, 0.1)}
    factors = {'L0_ffn_Wq': 8.0, 'L0_ffn_Wk': 8.0, 'L0_ffn_A': 8.0, 'L0_ffn_Bm': 8.0}
    for name, (base, spread) in spreads.items():
        noise = np.random.default_rng([zlib.crc32(name.encode()), seed]).standard_normal(out[name].shape)
        drawn = base * np.exp(spread * noise) if base else spread * noise
        out[name] = jnp.asarray(drawn.astype(out[name].dtype))
    for name, factor in factors.items():
        out[name] = (out[name] * factor).astype(out[name].dtype)
    return out
```

```python
from contextlib import ExitStack

import concourse.bass as bass
from concourse import mybir

ALU = mybir.AluOpType
ACT = mybir.ActivationFunctionType
F32 = mybir.dt.float32
F32R = mybir.dt.float32r
BF16 = mybir.dt.bfloat16
U8 = mybir.dt.uint8
AX_X = mybir.AxisListType.X

P = 128
B = 8
D = 512
C = D // P
H = 32
HG = 2
G = H // HG
NB = 4
HALF = B // 2
TOK = HALF * P
BLOCKS = G * NB
EPS = 1e-5
MASKED = 1e30
E, DK, R = 8, 32, 16
ER = E * R
QKA = 2 * E * DK + ER
HQ = QKA // 2
QK0, QK1, WV, WO = range(4)


def build(nc, x, ctx_t, mask, bias, ln_w, wq, wk, wv, wo, f_w, f_b, f_wq, f_wk, f_a, f_bm, out):
    with ExitStack() as ctx:
        def sb(name, shape, dt):
            return ctx.enter_context(nc.sbuf_tensor(name, shape, dt))

        def sem(name):
            return ctx.enter_context(nc.semaphore(name))

        x_hi = sb("x_hi", [P, C, B * P], F32R)
        x_lo = sb("x_lo", [P, C, B * P], F32R)
        c_hi = sb("c_hi", [P, C, B * P], F32R)
        c_lo = sb("c_lo", [P, C, B * P], F32R)
        resid = sb("resid", [P, B, D], F32)
        q_t = sb("q_t", [P, HG, B * P], F32)
        k_t = sb("k_t", [P, HG, B * P], F32)
        v_sb = sb("v_sb", [P, 2, B, HG * P], F32)
        at_hi = sb("at_hi", [P, HG, B * P], F32R)
        at_lo = sb("at_lo", [P, HG, B * P], F32R)
        raw = sb("raw", [P, 4, 1024], F32)
        wqk_hi = sb("wqk_hi", [P, HG, 2, C, P], F32R)
        wqk_lo = sb("wqk_lo", [P, HG, 2, C, P], F32R)
        wv_hi = sb("wv_hi", [P, 2, C, HG * P], F32R)
        wv_lo = sb("wv_lo", [P, 2, C, HG * P], F32R)
        wo_hi = sb("wo_hi", [P, 2, HG, D], F32R)
        wo_lo = sb("wo_lo", [P, 2, HG, D], F32R)
        bias_mask = sb("bias_mask", [P, 2, HALF, P], F32)
        mask_neg = sb("mask_neg", [P, B, P], BF16)
        bias_sb = sb("bias_sb", [P, 2, HG, P], F32)
        probs = sb("probs", [P, 2, HALF, P], F32)
        probs_t = sb("probs_t", [P, HALF * P], F32)
        ident = sb("ident", [P, P], F32)
        row_valid = sb("row_valid", [P, B], F32)
        neg_max = sb("neg_max", [P, 2, HALF], F32)
        row_sum = sb("row_sum", [P, 2, HALF], F32)
        row_inv = sb("row_inv", [P, 2, HALF], F32)
        ln_sb = sb("ln_sb", [P, C], F32)
        stats = sb("stats", [P, 6], F32)
        mean_var = sb("mean_var", [P, B, 2], F32)
        var_eps = sb("var_eps", [P, B], F32)
        rstd = sb("rstd", [P, B], F32)
        rms_inv = sb("rms_inv", [P, B], F32)
        minus_half = sb("minus_half", [P, B], F32)
        zero_bias = sb("zero_bias", [P, 1], F32)

        ctx_raw = [v_sb[:, 1].rearrange("p b n -> p (b n)").rearrange("p (c t) -> p c t", c=C),
                   q_t[:, :, :].rearrange("p h t -> p (h t)").rearrange("p (c t) -> p c t", c=C)]
        x_normed = v_sb[:, 1].rearrange("p b n -> p (b n)").rearrange("p (b d) -> p b d", b=HALF)
        mask_raw = probs_t[:, 0:B * P // 4].bitcast(U8)
        flat_v0 = v_sb[:, 0].rearrange("p b n -> p (b n)")
        flat_q = q_t[:, :, :].rearrange("p h t -> p (h t)")
        flat_k = k_t[:, :, :].rearrange("p h t -> p (h t)")
        fw_raw = raw[:, QK0:QK1 + 1].rearrange("p a n -> p (a n)").rearrange("p (c n) -> p c n", c=C)
        fq_raw = raw[:, WV].rearrange("p (c n) -> p c n", c=C)
        fk_raw = flat_v0[:, 0:1024].rearrange("p (c n) -> p c n", c=C)
        fa_raw = flat_v0[:, 1024:1536].rearrange("p (c n) -> p c n", c=C)
        bm_sb = flat_v0[:, 1536:2048]
        fb_sb = raw[:, WO, 0:D]
        y_sb = [flat_q[:, i * D:(i + 1) * D] for i in range(2)]
        resid_b = [flat_q[:, (2 + i) * D:(3 + i) * D] for i in range(2)]
        qka_sb = [flat_k[:, i * QKA:(i + 1) * QKA] for i in range(2)]
        prod = flat_k[:, 2 * QKA:2 * QKA + E * DK]
        at = 2 * QKA + E * DK
        u_sb = [flat_k[:, at + i * ER:at + (i + 1) * ER] for i in range(2)]
        u_t = [flat_k[:, at + (2 + i) * ER:at + (3 + i) * ER] for i in range(2)]
        router = sb("router", [P, 2, E], F32)
        router_e = sb("router_e", [P, 2, E], F32)
        router_nm = sb("router_nm", [P, 2], F32)
        router_sum = sb("router_sum", [P, 2], F32)
        router_inv = sb("router_inv", [P, 2], F32)

        def bank(name):
            return ctx.enter_context(nc.psum_tensor(name, [P, 512], F32))

        ps_q, ps_k, ps_v, ps_s, ps_pt, ps_pv, ps_o0, ps_o1 = [
            bank(n) for n in ("ps_q", "ps_k", "ps_v", "ps_s", "ps_pt", "ps_pv", "ps_o0", "ps_o1")]
        ps_o = (ps_o0, ps_o1)
        ps_w = (ps_q, ps_k)
        ps_a = (ps_s, ps_pt)
        ps_yt, ps_ut = ps_v, ps_pv

        ctx_in = [sem(f"ctx_in{i}") for i in range(2)]
        x_in = [sem(f"x_in{i}") for i in range(2)]
        small_in = sem("small_in")
        raw_in = [sem(f"raw_in{i}") for i in range(4)]
        bias_in = [sem("bias_in0"), sem("bias_in1")]
        ffn_in = sem("ffn_in")
        ffn_late_in = sem("ffn_late_in")
        bvec_in = sem("bvec_in")
        stored = sem("stored")
        w_hi_done = [sem(f"w_hi_done{i}") for i in range(4)]
        w_lo_done = [sem(f"w_lo_done{i}") for i in range(4)]
        f_hi_done = sem("f_hi_done")
        f_lo_done = sem("f_lo_done")
        ident_zero = sem("ident_zero")
        consts_ready = sem("consts_ready")
        mask_ready = sem("mask_ready")
        c_hi_done = sem("c_hi_done")
        c_lo_done = sem("c_lo_done")
        stats_done = sem("stats_done")
        aggr_done = sem("aggr_done")
        eps_added = sem("eps_added")
        rstd_done = sem("rstd_done")
        rms_a = sem("rms_a")
        rms_b = sem("rms_b")
        rms_done = sem("rms_done")
        hidden_done = sem("hidden_done")
        resid_done = sem("resid_done")
        normed_done = sem("normed_done")
        xt_done = sem("xt_done")
        x_hi_done = sem("x_hi_done")
        x_lo_done = sem("x_lo_done")
        q_done, k_done, v_done = sem("q_done"), sem("k_done"), sem("v_done")
        q_ready, k_ready, v_ready = sem("q_ready"), sem("k_ready"), sem("v_ready")
        bm_ready = sem("bm_ready")
        scores_done = sem("scores_done")
        scores_read = sem("scores_read")
        max_done = sem("max_done")
        exp_done = sem("exp_done")
        inv_done = sem("inv_done")
        probs_ready = sem("probs_ready")
        pt_done = sem("pt_done")
        pt_copied = sem("pt_copied")
        pv_done = sem("pv_done")
        at_hi_done = sem("at_hi_done")
        at_lo_done = sem("at_lo_done")
        o_done = sem("o_done")
        o_added = sem("o_added")
        f_stats, f_aggr, f_eps, f_rstd = sem("f_stats"), sem("f_aggr"), sem("f_eps"), sem("f_rstd")
        y_done, yt_done, yt_hi, yt_lo = sem("y_done"), sem("yt_done"), sem("yt_hi"), sem("yt_lo")
        resid_b_done = sem("resid_b_done")
        fa_done, fa_copied = sem("fa_done"), sem("fa_copied")
        prod_done, route_sum, route_scaled = sem("prod_done"), sem("route_sum"), sem("route_scaled")
        route_max, route_exp, route_inv = sem("route_max"), sem("route_exp"), sem("route_inv")
        u_done, ut_done, ut_copied = sem("u_done"), sem("ut_done"), sem("ut_copied")
        fo_done, result_done = sem("fo_done"), sem("result_done")

        def per_group(engine, step):
            step(0, 0)
            with engine.Fori(1, G - 4, 2) as g:
                step(g, 1)
                step(g + 1, 0)
            for g in range(G - 3, G):
                step(g, g % 2)

        def exists(group):
            return not isinstance(group, int) or group < G

        block = ctx.enter_context(nc.Block())

        @block.sync
        def _(sp):
            def load(kind, g):
                if kind in (QK0, QK1):
                    h = HG * g + kind
                    sp.dma_start(raw[:, kind, 0:512], wq[h]).then_inc(raw_in[kind], 16)
                    sp.dma_start(raw[:, kind, 512:1024], wk[h]).then_inc(raw_in[kind], 16)
                elif kind == WV:
                    sp.dma_start(raw[:, WV, :], wv[g]).then_inc(raw_in[WV], 16)
                else:
                    sp.dma_start(raw[:, WO, :], wo[g]).then_inc(raw_in[WO], 16)

            def load_bias(g, p):
                sp.dma_start(bias_sb[:, p], bias[g]).then_inc(bias_in[p], 16)

            sp.dma_start(ctx_raw[0], ctx_t[:, 0]).then_inc(ctx_in[0], 16)
            load(QK0, 0)
            load(WV, 0)
            load(QK1, 0)
            sp.dma_start(ctx_raw[1], ctx_t[:, 1]).then_inc(ctx_in[1], 16)
            sp.dma_start(mask_raw, mask).then_inc(small_in, 16)
            sp.dma_start(ln_sb[:, :], ln_w).then_inc(small_in, 16)
            load_bias(0, 0)
            load_bias(1, 1)
            sp.wait_ge(w_lo_done[WV], 1)
            load(WV, 1)
            sp.wait_ge(w_lo_done[QK0], 1)
            load(QK0, 1)
            sp.wait_ge(w_lo_done[QK1], 1)
            load(QK1, 1)
            load(WO, 0)
            sp.wait_ge(w_lo_done[WV], 2)
            load(WV, 2)
            sp.wait_ge(w_lo_done[QK0], 2)
            load(QK0, 2)

            def step(g, p):
                if exists(g + 2):
                    sp.wait_ge(w_lo_done[QK1], g + 2)
                    load(QK1, g + 2)
                if exists(g + 3):
                    sp.wait_ge(w_lo_done[WV], g + 3)
                    load(WV, g + 3)
                if exists(g + 1):
                    sp.wait_ge(w_lo_done[WO], g + 1)
                    load(WO, g + 1)
                if exists(g + 2):
                    sp.wait_ge(bm_ready, NB * g + NB)
                    load_bias(g + 2, p)
                if exists(g + 3):
                    sp.wait_ge(w_lo_done[QK0], g + 3)
                    load(QK0, g + 3)
                if isinstance(g, int) and g == G - 2:
                    sp.wait_ge(w_lo_done[QK0], G)
                    sp.wait_ge(w_lo_done[QK1], G)
                    sp.wait_ge(w_lo_done[WV], G)
                    sp.dma_start(fw_raw, f_w).then_inc(ffn_in, 16)
                    sp.dma_start(fq_raw, f_wq).then_inc(ffn_in, 16)
                    sp.wait_ge(pv_done, BLOCKS - NB)
                    sp.dma_start(fk_raw, f_wk).then_inc(ffn_late_in, 16)
                    sp.dma_start(fa_raw, f_a).then_inc(ffn_late_in, 16)
                    sp.dma_start(bm_sb, f_bm).then_inc(ffn_late_in, 16)
                if isinstance(g, int) and g == G - 1:
                    sp.wait_ge(w_lo_done[WO], G)
                    sp.dma_start(fb_sb, f_b.to_broadcast([P, D])).then_inc(bvec_in, 16)

            per_group(sp, step)
            for b in range(B):
                sp.wait_ge(result_done, b + 1)
                sp.dma_start(out[b], resid[:, b, :]).then_inc(stored, 16)
            sp.wait_ge(stored, 16 * B)

        @block.gpsimd
        def _(pool):
            nc.gpsimd.memset(ident[:, :], 0.0).then_inc(ident_zero, 1)
            pool.wait_ge(ident_zero, 1)
            nc.gpsimd.affine_select(out=ident[:, :], in_=ident[:, :], compare_op=ALU.not_equal, fill=1.0,
                                    base=0, pattern=[[-1, P]], channel_multiplier=1).then_inc(consts_ready, 1)
            nc.gpsimd.memset(minus_half[:, :], -0.5).then_inc(consts_ready, 1)
            pool.wait_ge(consts_ready, 2)
            for half in range(2):
                bs = slice(HALF * half, HALF * (half + 1))
                pool.wait_ge(eps_added, half + 1)
                nc.gpsimd.tensor_tensor(rstd[:, bs], var_eps[:, bs], minus_half[:, bs], ALU.pow).then_inc(rstd_done, 1)
                pool.wait_ge(rms_b, half + 1)
                nc.gpsimd.tensor_tensor(rms_inv[:, bs], rms_inv[:, bs], minus_half[:, bs], ALU.pow).then_inc(rms_done, 1)
                for b in range(HALF * half, HALF * (half + 1)):
                    pool.wait_ge(hidden_done, b + 1)
                    nc.gpsimd.tensor_tensor(resid[:, b, :], resid[:, b, :],
                                            probs[:, b % 2].rearrange("p b n -> p (b n)"), ALU.add).then_inc(resid_done, 1)
            pool.wait_ge(mask_ready, 1)

            def bias_and_mask(s, g, j, p):
                if not isinstance(s, int) or s >= 2:
                    pool.wait_ge(scores_read, s - 1)
                head, half = j % 2, j // 2
                one = bias_sb[:, p, head:head + 1, :].to_broadcast([P, HALF, P])
                nc.gpsimd.tensor_tensor(bias_mask[:, j % 2], one,
                                        mask_neg[:, HALF * half:HALF * (half + 1), :], ALU.add).then_inc(bm_ready, 1)

            def step(g, p):
                if isinstance(g, int):
                    pool.wait_ge(bias_in[p], 16 * (g // 2 + 1))
                else:
                    pool.wait_ge(bias_in[p], 8 * (g - p) + 16)
                for j in range(NB):
                    bias_and_mask(NB * g + j, g, j, p)

            per_group(pool, step)
            pool.wait_ge(bvec_in, 16)

            def inverse_deviation(b):
                pool.wait_ge(f_eps, b + 1)
                nc.gpsimd.tensor_tensor(rstd[:, b:b + 1], var_eps[:, b:b + 1], minus_half[:, 0:1], ALU.pow).then_inc(f_rstd, 1)

            inverse_deviation(0)
            inverse_deviation(1)
            for b in range(B):
                if b >= 2:
                    pool.wait_ge(result_done, b - 1)
                nc.gpsimd.tensor_tensor(resid_b[b % 2], resid[:, b, :], fb_sb, ALU.add).then_inc(resid_b_done, 1)
                if b + 2 < B:
                    inverse_deviation(b + 2)

        def weight_parts(kind, p):
            def flat(t):
                names = " ".join("abcd"[:len(t.shape) - 1])
                return t.rearrange(f"p {names} -> p ({names})")
            if kind in (QK0, QK1):
                return raw[:, kind], flat(wqk_hi[:, kind]), flat(wqk_lo[:, kind])
            if kind == WV:
                return raw[:, WV], flat(wv_hi[:, p]), flat(wv_lo[:, p])
            return raw[:, WO], flat(wo_hi[:, p]), flat(wo_lo[:, p])

        def slot_weights(j, g, p):
            return [(QK1, g + 1, 0), (WV, g + 2, p), (WO, g, p), (QK0, g + 2, 0)][j]

        loads_of = {QK0: 2, QK1: 2, WV: 1, WO: 1}

        def ffn_parts(n):
            if n < 2:
                cs = slice(2 * n, 2 * n + 2)
                return [(fw_raw[:, cs, :], x_hi[:, cs, 0:D], x_lo[:, cs, 0:D])]
            if n == 2:
                return [(fq_raw, c_hi[:, :, 0:E * DK], c_lo[:, :, 0:E * DK])]
            return [(fk_raw, c_hi[:, :, E * DK:2 * E * DK], c_lo[:, :, E * DK:2 * E * DK]),
                    (fa_raw, c_hi[:, :, 2 * E * DK:QKA], c_lo[:, :, 2 * E * DK:QKA])]

        @block.scalar
        def _(act):
            def copy(o, i):
                return nc.scalar.activation(o, i, ACT.Copy)

            def split_hi(kind, group, p):
                act.wait_ge(raw_in[kind], 16 * loads_of[kind] * (group + 1))
                r, hi, _ = weight_parts(kind, p)
                copy(hi, r).then_inc(w_hi_done[kind], 1)

            def q_out(n, j):
                act.wait_ge(q_done, n + 1)
                copy(q_t[:, j % 2, TOK * (j // 2):TOK * (j // 2 + 1)], ps_q[:, :]).then_inc(q_ready, 1)

            def k_out(n, j):
                act.wait_ge(k_done, n + 1)
                copy(k_t[:, j % 2, TOK * (j // 2):TOK * (j // 2 + 1)], ps_k[:, :]).then_inc(k_ready, 1)

            def v_out(n, j, p):
                act.wait_ge(v_done, n + 1)
                copy(v_sb[:, p, 2 * j:2 * j + 2, :].rearrange("p b n -> p (b n)"), ps_v[:, :]).then_inc(v_ready, 1)

            for half in range(2):
                act.dma_start(resid[:, HALF * half:HALF * (half + 1), :],
                              x[HALF * half:HALF * (half + 1)].rearrange("b p d -> p b d")).then_inc(x_in[half], 16)
            act.wait_ge(ctx_in[0], 16)
            copy(c_hi[:, :, 0:TOK], ctx_raw[0]).then_inc(c_hi_done, 1)
            split_hi(QK0, 0, 0)
            split_hi(WV, 0, 0)
            k_out(0, 0)
            split_hi(QK1, 0, 0)
            v_out(0, 0, 0)
            act.wait_ge(ctx_in[1], 16)
            copy(c_hi[:, :, TOK:2 * TOK], ctx_raw[1]).then_inc(c_hi_done, 1)

            def normed(b):
                act.wait_ge(rms_done, b // HALF + 1)
                act.wait_ge(hidden_done, b + 1)
                if b == 0:
                    act.wait_ge(c_lo_done, 1)
                if b == HALF:
                    act.wait_ge(xt_done, C)
                nc.scalar.activation(x_normed[:, b % HALF, :], probs[:, b % 2].rearrange("p b n -> p (b n)"),
                                     ACT.Copy, scale=rms_inv[:, b:b + 1]).then_inc(normed_done, 1)

            def x_high(n):
                half, c = n // C, n % C
                if n == 0:
                    act.wait_ge(small_in, 32)
                act.wait_ge(xt_done, n + 1)
                nc.scalar.activation(x_hi[:, c, TOK * half:TOK * (half + 1)], ps_o[n % 2][:, :], ACT.Copy,
                                     scale=ln_sb[:, c:c + 1]).then_inc(x_hi_done, 1)

            k_out(1, 1)
            v_out(1, 1, 0)
            for b in range(HALF):
                normed(b)
            k_out(2, 2)
            for n in range(C):
                x_high(n)
            v_out(2, 2, 0)
            for b in range(HALF, B):
                normed(b)
            k_out(3, 3)
            v_out(3, 3, 0)
            for n in range(C, 2 * C):
                x_high(n)
            split_hi(WV, 1, 1)
            for j in range(3):
                q_out(j, j)
            split_hi(QK0, 1, 0)
            q_out(3, 3)

            def step(g, p):
                s0 = NB * g
                last = isinstance(g, int) and g == G - 1
                for j in range(NB):
                    s = s0 + j
                    kind, group, wp = slot_weights(j, g, p)
                    if exists(group):
                        if kind in (QK0, QK1):
                            act.wait_ge(k_done, s + 4)
                        elif kind == WV:
                            act.wait_ge(v_done, s + 3)
                        elif not isinstance(g, int) or g >= 2:
                            act.wait_ge(o_done, s - 6)
                        split_hi(kind, group, wp)
                    if last:
                        if j == 0:
                            act.wait_ge(v_done, BLOCKS)
                            act.wait_ge(ffn_in, 16 * 2)
                        if j == NB - 1:
                            act.wait_ge(ffn_late_in, 16 * 3)
                        for r, hi, _ in ffn_parts(j):
                            copy(hi, r).then_inc(f_hi_done, 1)
                    act.wait_ge(max_done, s + 1)
                    for i in range(HALF):
                        e = nc.scalar.activation(probs[:, j % 2, i, :], probs[:, j % 2, i, :], ACT.Exp,
                                                 bias=neg_max[:, j % 2, i:i + 1],
                                                 accum_out=row_sum[:, j % 2, i:i + 1])
                    e.then_inc(exp_done, 1)
                    if j > 0 or not isinstance(g, int) or g > 0:
                        act.wait_ge(pt_done, s)
                        copy(probs_t[:, :], ps_pt[:, :]).then_inc(pt_copied, 1)
                    if not last:
                        q_out(s + NB, j)
                        k_out(s + NB, j)
                    if j > 0 or not isinstance(g, int) or g > 0:
                        at_high(s, j)
                    if not last:
                        v_out(s + NB, j, 1 - p)

            def at_high(s, j):
                jj = (j - 1) % NB
                act.wait_ge(pv_done, s)
                copy(at_hi[:, jj % 2, TOK * (jj // 2):TOK * (jj // 2 + 1)], ps_pv[:, :]).then_inc(at_hi_done, 1)

            per_group(act, step)
            act.wait_ge(pt_done, BLOCKS)
            copy(probs_t[:, :], ps_pt[:, :]).then_inc(pt_copied, 1)
            at_high(BLOCKS, 0)

            def yt_high(b):
                act.wait_ge(yt_done, b + 1)
                copy(x_hi[:, :, D + P * (b % 2):D + P * (b % 2 + 1)],
                     ps_yt[:, :].rearrange("p (c t) -> p c t", c=C)).then_inc(yt_hi, 1)

            yt_high(0)
            for b in range(B):
                act.wait_ge(fa_done, b + 1)
                if b >= 2:
                    act.wait_ge(u_done, b - 1)
                for i in range(2):
                    a = copy(qka_sb[b % 2][:, HQ * i:HQ * (i + 1)], ps_a[i][:, 0:HQ])
                a.then_inc(fa_copied, 1)
                if b + 1 < B:
                    yt_high(b + 1)
                act.wait_ge(route_max, b + 1)
                nc.scalar.activation(router_e[:, b % 2, :], router[:, b % 2, :], ACT.Exp,
                                     bias=router_nm[:, b % 2:b % 2 + 1],
                                     accum_out=router_sum[:, b % 2:b % 2 + 1]).then_inc(route_exp, 1)
                act.wait_ge(ut_done, b + 1)
                copy(u_t[b % 2], ps_ut[:, 0:P]).then_inc(ut_copied, 1)

        @block.vector
        def _(dve):
            def sub(o, a, hi):
                return nc.vector.tensor_tensor(o, a, hi.bitcast(F32), ALU.subtract)

            def split_lo(kind, group, p):
                dve.wait_ge(w_hi_done[kind], group + 1)
                r, hi, lo = weight_parts(kind, p)
                sub(lo, r, hi).then_inc(w_lo_done[kind], 1)

            dve.wait_ge(c_hi_done, 1)
            sub(c_lo[:, :, 0:TOK], ctx_raw[0], c_hi[:, :, 0:TOK]).then_inc(c_lo_done, 1)
            split_lo(QK0, 0, 0)
            split_lo(WV, 0, 0)
            split_lo(QK1, 0, 0)
            dve.wait_ge(c_hi_done, 2)
            sub(c_lo[:, :, TOK:2 * TOK], ctx_raw[1], c_hi[:, :, TOK:2 * TOK]).then_inc(c_lo_done, 1)

            def tile_stats(b, n, done, aggregated):
                if n > 0:
                    dve.wait_ge(aggregated, n)
                nc.vector.bn_stats(stats[:, :], resid[:, b, :]).then_inc(done, 1)
                dve.wait_ge(done, n + 1)
                nc.vector.bn_aggr(mean_var[:, b, :], stats[:, :]).then_inc(aggregated, 1)

            def x_low(n):
                half, c = n // C, n % C
                ts = slice(TOK * half, TOK * (half + 1))
                dve.wait_ge(x_hi_done, n + 1)
                nc.vector.scalar_tensor_tensor(out=x_lo[:, c, ts], in0=ps_o[n % 2][:, :], scalar=ln_sb[:, c:c + 1],
                                               in1=x_hi[:, c, ts].bitcast(F32), op0=ALU.mult,
                                               op1=ALU.subtract).then_inc(x_lo_done, 1)

            for half in range(2):
                bs = slice(HALF * half, HALF * (half + 1))
                dve.wait_ge(x_in[half], 16)
                for b in range(HALF * half, HALF * (half + 1)):
                    tile_stats(b, b, stats_done, aggr_done)
                dve.wait_ge(aggr_done, HALF * (half + 1))
                nc.vector.tensor_scalar(var_eps[:, bs], mean_var[:, bs, 1], EPS, None, ALU.add).then_inc(eps_added, 1)
                dve.wait_ge(rstd_done, half + 1)
                nc.vector.tensor_tensor(rms_inv[:, bs], rstd[:, bs], rstd[:, bs], ALU.mult).then_inc(rms_a, 1)
                dve.wait_ge(rms_a, 2 * half + 1)
                nc.vector.tensor_tensor(rms_inv[:, bs], rms_inv[:, bs], mean_var[:, bs, 1], ALU.mult).then_inc(rms_a, 1)
                dve.wait_ge(rms_a, 2 * half + 2)
                nc.vector.tensor_scalar(rms_inv[:, bs], rms_inv[:, bs], EPS, None, ALU.add).then_inc(rms_b, 1)
                for b in range(HALF * half, HALF * (half + 1)):
                    if b >= 2:
                        dve.wait_ge(resid_done, b - 1)
                        dve.wait_ge(normed_done, b - 1)
                    nc.vector.tensor_scalar(probs[:, b % 2].rearrange("p b n -> p (b n)"), resid[:, b, :],
                                            mean_var[:, b, 0:1], rstd[:, b:b + 1],
                                            ALU.subtract, ALU.mult).then_inc(hidden_done, 1)
                if half == 0:
                    dve.wait_ge(small_in, 32)
                    nc.vector.tensor_scalar(mask_neg[:, :, :].rearrange("p b k -> p (b k)"), mask_raw, -1.0, MASKED,
                                            ALU.add, ALU.mult).then_inc(mask_ready, 1)
                    nc.vector.tensor_reduce(row_valid[:, :], mask_raw.rearrange("p (b k) -> p b k", b=B),
                                            AX_X, ALU.max).then_inc(mask_ready, 1)
                for n in range(C * half, C * (half + 1)):
                    x_low(n)
            split_lo(WV, 1, 1)
            split_lo(QK0, 1, 0)
            dve.wait_ge(mask_ready, 2)
            dve.wait_ge(resid_done, B)
            dve.wait_ge(normed_done, B)

            def add_output(n, j):
                dve.wait_ge(o_done, n + 1)
                for i in range(2):
                    a = nc.vector.tensor_tensor(resid[:, 2 * j + i, :], ps_o[i][:, :], resid[:, 2 * j + i, :], ALU.add)
                a.then_inc(o_added, 1)

            def at_low(s, j):
                jj = (j - 1) % NB
                ts = slice(TOK * (jj // 2), TOK * (jj // 2 + 1))
                dve.wait_ge(at_hi_done, s)
                sub(at_lo[:, jj % 2, ts], ps_pv[:, :], at_hi[:, jj % 2, ts]).then_inc(at_lo_done, 1)

            def step(g, p):
                later = not isinstance(g, int) or g > 0
                for j in range(NB):
                    s = NB * g + j
                    half = j // 2
                    pr = probs[:, j % 2]
                    dve.wait_ge(scores_done, s + 1)
                    dve.wait_ge(bm_ready, s + 1)
                    nc.vector.tensor_tensor(pr, ps_s[:, :].rearrange("p (b k) -> p b k", b=HALF),
                                            bias_mask[:, j % 2], ALU.add).then_inc(scores_read, 1)
                    dve.wait_ge(scores_read, s + 1)
                    nc.vector.tensor_reduce(neg_max[:, j % 2, :], pr, AX_X, ALU.max, negate=True).then_inc(max_done, 1)
                    if later:
                        add_output(s - 4, j)
                    kind, group, wp = slot_weights(j, g, p)
                    if exists(group):
                        split_lo(kind, group, wp)
                    if isinstance(g, int) and g == G - 1:
                        for i, (r, hi, lo) in enumerate(ffn_parts(j)):
                            dve.wait_ge(f_hi_done, j + i + 1)
                            sub(lo, r, hi).then_inc(f_lo_done, 1)
                    dve.wait_ge(exp_done, s + 1)
                    nc.vector.reciprocal(row_inv[:, j % 2, :], row_sum[:, j % 2, :]).then_inc(inv_done, 1)
                    dve.wait_ge(inv_done, s + 1)
                    for i in range(HALF):
                        b = HALF * half + i
                        n = nc.vector.tensor_scalar(pr[:, i, :], pr[:, i, :], row_inv[:, j % 2, i:i + 1],
                                                    row_valid[:, b:b + 1], ALU.mult, ALU.mult)
                    n.then_inc(probs_ready, 1)
                    if later or j > 0:
                        at_low(s, j)

            per_group(dve, step)

            def normalise(b):
                tile_stats(b, b, f_stats, f_aggr)
                dve.wait_ge(f_aggr, b + 1)
                nc.vector.tensor_scalar(var_eps[:, b:b + 1], mean_var[:, b, 1:2], EPS, None, ALU.add).then_inc(f_eps, 1)

            def normalised(b):
                dve.wait_ge(f_rstd, b + 1)
                if b >= 2:
                    dve.wait_ge(yt_done, b - 1)
                nc.vector.tensor_scalar(y_sb[b % 2], resid[:, b, :], mean_var[:, b, 0:1], rstd[:, b:b + 1],
                                        ALU.subtract, ALU.mult).then_inc(y_done, 1)

            def yt_low(b):
                ts = slice(D + P * (b % 2), D + P * (b % 2 + 1))
                dve.wait_ge(yt_hi, b + 1)
                sub(x_lo[:, :, ts], ps_yt[:, :].rearrange("p (c t) -> p c t", c=C), x_hi[:, :, ts]).then_inc(yt_lo, 1)

            def result(b):
                dve.wait_ge(fo_done, b + 1)
                dve.wait_ge(resid_b_done, b + 1)
                nc.vector.tensor_tensor(resid[:, b, :], ps_w[b % 2][:, :], resid_b[b % 2],
                                        ALU.add).then_inc(result_done, 1)

            add_output(BLOCKS - 4, 0)
            dve.wait_ge(o_added, BLOCKS - 3)
            normalise(0)
            at_low(BLOCKS, 0)
            add_output(BLOCKS - 3, 1)
            normalised(0)
            dve.wait_ge(o_added, BLOCKS - 2)
            normalise(1)
            yt_low(0)
            normalised(1)
            add_output(BLOCKS - 2, 2)
            add_output(BLOCKS - 1, 3)
            dve.wait_ge(o_added, BLOCKS)
            for b in range(B):
                if b + 1 < B:
                    yt_low(b + 1)
                if b + 2 < B:
                    normalise(b + 2)
                q = b % 2
                dve.wait_ge(fa_copied, b + 1)
                nc.vector.tensor_tensor(prod, qka_sb[q][:, 0:E * DK], qka_sb[q][:, E * DK:2 * E * DK],
                                        ALU.mult).then_inc(prod_done, 1)
                dve.wait_ge(prod_done, b + 1)
                nc.vector.tensor_reduce(router[:, q, :], prod.rearrange("p (e d) -> p e d", e=E),
                                        AX_X, ALU.add).then_inc(route_sum, 1)
                dve.wait_ge(route_sum, b + 1)
                nc.vector.tensor_scalar(router[:, q, :], router[:, q, :], float(DK) ** -0.5, None,
                                        ALU.mult).then_inc(route_scaled, 1)
                dve.wait_ge(route_scaled, b + 1)
                nc.vector.tensor_reduce(router_nm[:, q:q + 1], router[:, q, :], AX_X, ALU.max,
                                        negate=True).then_inc(route_max, 1)
                if b + 2 < B:
                    normalised(b + 2)
                dve.wait_ge(route_exp, b + 1)
                nc.vector.reciprocal(router_inv[:, q:q + 1], router_sum[:, q:q + 1]).then_inc(route_inv, 1)
                dve.wait_ge(route_inv, b + 1)
                nc.vector.scalar_tensor_tensor(
                    out=u_sb[q].rearrange("p (e r) -> p e r", e=E),
                    in0=qka_sb[q][:, 2 * E * DK:QKA].rearrange("p (e r) -> p e r", e=E),
                    scalar=router_inv[:, q:q + 1],
                    in1=router_e[:, q, :].rearrange("p (e o) -> p e o", o=1).to_broadcast([P, E, R]),
                    op0=ALU.mult, op1=ALU.mult).then_inc(u_done, 1)
                if b > 0:
                    result(b - 1)
            result(B - 1)

        @block.tensor
        def _(pe):
            def passes(o, terms):
                for n, (lh, ll, rh, rl) in enumerate(terms):
                    pe.matmul(o, lh, rh, start=(n == 0), stop=False)
                    pe.matmul(o, lh, rl, start=False, stop=False)
                    m = pe.matmul(o, ll, rh, start=False, stop=(n == len(terms) - 1))
                return m

            def project(o, which, head, a_hi, a_lo, half):
                ts = slice(TOK * half, TOK * (half + 1))
                return passes(o, [(wqk_hi[:, head, which, c, :], wqk_lo[:, head, which, c, :],
                                   a_hi[:, c, ts], a_lo[:, c, ts]) for c in range(C)])

            def q_block(n, j, weights):
                if j < 2:
                    pe.wait_ge(w_lo_done[QK0 + j % 2], weights)
                if not isinstance(n, int) or n > 0:
                    pe.wait_ge(q_ready, n)
                project(ps_q[:, :], 0, j % 2, x_hi, x_lo, j // 2).then_inc(q_done, 1)

            def k_block(n, j):
                if not isinstance(n, int) or n > 0:
                    pe.wait_ge(k_ready, n)
                project(ps_k[:, :], 1, j % 2, c_hi, c_lo, j // 2).then_inc(k_done, 1)

            def v_block(n, j, p, weights):
                if j == 0:
                    pe.wait_ge(w_lo_done[WV], weights)
                if not isinstance(n, int) or n > 0:
                    pe.wait_ge(v_ready, n)
                for i in range(2):
                    ts = slice(P * (2 * j + i), P * (2 * j + i + 1))
                    m = passes(ps_v[:, HG * P * i:HG * P * (i + 1)],
                               [(c_hi[:, c, ts], c_lo[:, c, ts], wv_hi[:, p, c, :], wv_lo[:, p, c, :])
                                for c in range(C)])
                m.then_inc(v_done, 1)

            def x_transposes(half):
                pe.wait_ge(normed_done, HALF * (half + 1))
                for c in range(C):
                    n = C * half + c
                    if n >= 2:
                        pe.wait_ge(x_lo_done, n - 1)
                    for i in range(HALF):
                        m = pe.transpose(ps_o[n % 2][:, P * i:P * (i + 1)], x_normed[:, i, P * c:P * (c + 1)],
                                         ident[:, :])
                    m.then_inc(xt_done, 1)

            pe.wait_ge(consts_ready, 2)
            pe.wait_ge(c_lo_done, 1)
            pe.wait_ge(w_lo_done[QK0], 1)
            k_block(0, 0)
            v_block(0, 0, 0, 1)
            pe.wait_ge(w_lo_done[QK1], 1)
            k_block(1, 1)
            v_block(1, 1, 0, 1)
            pe.wait_ge(c_lo_done, 2)
            k_block(2, 2)
            x_transposes(0)
            v_block(2, 2, 0, 1)
            k_block(3, 3)
            v_block(3, 3, 0, 1)
            x_transposes(1)
            pe.wait_ge(x_lo_done, C)
            q_block(0, 0, 1)
            q_block(1, 1, 1)
            pe.wait_ge(x_lo_done, 2 * C)
            q_block(2, 2, 1)
            q_block(3, 3, 1)

            def scores(s, j):
                head, half = j % 2, j // 2
                pe.wait_ge(q_ready, s + 1)
                pe.wait_ge(k_ready, s + 1)
                if not isinstance(s, int) or s > 0:
                    pe.wait_ge(scores_read, s)
                for i in range(HALF):
                    ts = slice(TOK * half + P * i, TOK * half + P * (i + 1))
                    m = pe.matmul(ps_s[:, P * i:P * (i + 1)], q_t[:, head, ts], k_t[:, head, ts],
                                  start=True, stop=True)
                m.then_inc(scores_done, 1)

            def turn_probs(s, j):
                pe.wait_ge(probs_ready, s)
                if not isinstance(s, int) or s > 1:
                    pe.wait_ge(pt_copied, s - 1)
                for i in range(HALF):
                    m = pe.transpose(ps_pt[:, P * i:P * (i + 1)], probs[:, (j - 1) % 2, i, :], ident[:, :])
                m.then_inc(pt_done, 1)

            def probs_v(s, j, p):
                jj = (j - 1) % NB
                vp = p if j > 0 else 1 - p
                pe.wait_ge(pt_copied, s)
                pe.wait_ge(v_ready, s - jj + 1 + 2 * (jj // 2))
                if not isinstance(s, int) or s > 1:
                    pe.wait_ge(at_lo_done, s - 1)
                for i in range(HALF):
                    m = pe.matmul(ps_pv[:, P * i:P * (i + 1)],
                                  v_sb[:, vp, HALF * (jj // 2) + i, P * (jj % 2):P * (jj % 2 + 1)],
                                  probs_t[:, P * i:P * (i + 1)], start=True, stop=True)
                m.then_inc(pv_done, 1)

            def output_pair(n, j, p, weights=0):
                nj = (j + 1) % NB
                wp = p if j == 3 else 1 - p
                if nj == 0:
                    pe.wait_ge(w_lo_done[WO], weights)
                pe.wait_ge(at_lo_done, n - nj + 2 + 2 * (nj // 2))
                if not isinstance(n, int) or n > 0:
                    pe.wait_ge(o_added, n)
                for i in range(2):
                    ts = slice(P * (2 * nj + i), P * (2 * nj + i + 1))
                    m = passes(ps_o[i][:, :], [(at_hi[:, h, ts], at_lo[:, h, ts], wo_hi[:, wp, h, :],
                                                wo_lo[:, wp, h, :]) for h in range(HG)])
                m.then_inc(o_done, 1)

            def step(g, p):
                first = isinstance(g, int) and g == 0
                last = isinstance(g, int) and g == G - 1
                for j in range(NB):
                    s = NB * g + j
                    scores(s, j)
                    if not last:
                        q_block(s + NB, j, g + 2)
                    if not first or j > 0:
                        turn_probs(s, j)
                    if not last:
                        k_block(s + NB, j)
                    if not first or j > 0:
                        probs_v(s, j, p)
                    if not last:
                        v_block(s + NB, j, 1 - p, g + 2)
                    if not first or j == 3:
                        output_pair(s - 3, j, p, g + 1)

            per_group(pe, step)
            turn_probs(BLOCKS, 0)
            output_pair(BLOCKS - 3, 0, 0)
            probs_v(BLOCKS, 0, 0)

            def y_transposes(b):
                pe.wait_ge(y_done, b + 1)
                if b > 0:
                    pe.wait_ge(yt_lo, b)
                for c in range(C):
                    m = pe.transpose(ps_yt[:, P * c:P * (c + 1)], y_sb[b % 2][:, P * c:P * (c + 1)], ident[:, :])
                m.then_inc(yt_done, 1)

            def yt(b):
                ts = slice(D + P * (b % 2), D + P * (b % 2 + 1))
                return [(x_hi[:, c, ts], x_lo[:, c, ts]) for c in range(C)]

            y_transposes(0)
            output_pair(BLOCKS - 2, 1, 0)
            output_pair(BLOCKS - 1, 2, 0)
            y_transposes(1)
            pe.wait_ge(f_lo_done, 5)
            for b in range(B):
                pe.wait_ge(yt_lo, b + 1)
                if b > 0:
                    pe.wait_ge(fa_copied, b)
                for i in range(2):
                    ns = slice(HQ * i, HQ * (i + 1))
                    m = passes(ps_a[i][:, 0:HQ], [(*yt(b)[c], c_hi[:, c, ns], c_lo[:, c, ns]) for c in range(C)])
                m.then_inc(fa_done, 1)
                if b > 0:
                    pe.wait_ge(u_done, b)
                    pe.transpose(ps_ut[:, 0:P], u_sb[(b - 1) % 2], ident[:, :]).then_inc(ut_done, 1)
                if b >= 2:
                    pe.wait_ge(result_done, b - 1)
                for c in range(C):
                    yh, yl = yt(b)[c]
                    pe.matmul(ps_w[b % 2][:, :], yh, x_hi[:, c, 0:D], start=(c == 0), stop=False)
                    pe.matmul(ps_w[b % 2][:, :], yh, x_lo[:, c, 0:D], start=False, stop=False)
                    pe.matmul(ps_w[b % 2][:, :], yl, x_hi[:, c, 0:D], start=False, stop=False)
                if b > 0:
                    pe.wait_ge(ut_copied, b)
                    pe.matmul(ps_w[(b - 1) % 2][:, :], u_t[(b - 1) % 2], bm_sb, start=False,
                              stop=True).then_inc(fo_done, 1)
                if b + 2 < B:
                    y_transposes(b + 2)
            b = B - 1
            pe.wait_ge(u_done, b + 1)
            pe.transpose(ps_ut[:, 0:P], u_sb[b % 2], ident[:, :]).then_inc(ut_done, 1)
            pe.wait_ge(ut_copied, b + 1)
            pe.matmul(ps_w[b % 2][:, :], u_t[b % 2], bm_sb, start=False, stop=True).then_inc(fo_done, 1)


def kernel(x, ctx_4096, mask_BxSxS2_bk0, L0_xattn_position_bias, L0_xattn_ln_weight, L0_xattn_w_q,
           L0_xattn_w_k, L0_xattn_w_v, L0_xattn_w_out, L0_ffn_W, L0_ffn_b, L0_ffn_Wq, L0_ffn_Wk,
           L0_ffn_A, L0_ffn_Bm):
    import numpy as np
    import concourse.bacc as bacc
    from concourse.bass_utils import run_bass_kernel_spmd

    def heads(w):
        return np.asarray(w).reshape(H, P, C, P).transpose(0, 3, 2, 1).reshape(H, P, C * P)

    def turned(w):
        w = np.asarray(w)
        return w.reshape(w.shape[0], C, P).transpose(2, 1, 0)

    laid = {
        "x": np.asarray(x),
        "ctx_t": np.asarray(ctx_4096).reshape(2, TOK, C, P).transpose(3, 0, 2, 1),
        "mask": np.asarray(mask_BxSxS2_bk0).transpose(1, 0, 2).reshape(P, B * P),
        "bias": np.asarray(L0_xattn_position_bias).reshape(G, HG, P, P).transpose(0, 2, 1, 3),
        "ln_w": np.asarray(L0_xattn_ln_weight).reshape(C, P).T,
        "wq": heads(L0_xattn_w_q),
        "wk": heads(L0_xattn_w_k),
        "wv": np.asarray(L0_xattn_w_v).reshape(G, HG * P, C, P).transpose(0, 3, 2, 1).reshape(G, P, C * HG * P),
        "wo": np.asarray(L0_xattn_w_out).reshape(D, G, HG, P).transpose(1, 3, 2, 0).reshape(G, P, HG * D),
        "f_w": turned(L0_ffn_W),
        "f_b": np.asarray(L0_ffn_b).reshape(1, D),
        "f_wq": turned(L0_ffn_Wq),
        "f_wk": turned(L0_ffn_Wk),
        "f_a": turned(np.asarray(L0_ffn_A).reshape(ER, D)),
        "f_bm": np.asarray(L0_ffn_Bm).transpose(0, 2, 1).reshape(ER, D),
    }
    nc = bacc.Bacc("TRN2", target_bir_lowering=False, num_devices=1)
    arrays, args = {}, []
    for name, a in laid.items():
        a = np.ascontiguousarray(a)
        arrays[name] = a
        args.append(nc.dram_tensor(name, a.shape, mybir.dt.from_np(a.dtype), kind="ExternalInput").ap())
    result = nc.dram_tensor("out", (B, P, D), F32, kind="ExternalOutput").ap()
    build(nc, *args, result)
    r = run_bass_kernel_spmd(nc, [arrays], core_ids=[0])
    return r.results[0]["out"]
```

```python
from contextlib import ExitStack

import concourse.bass as bass
from concourse import mybir

ALU = mybir.AluOpType
ACT = mybir.ActivationFunctionType
F32 = mybir.dt.float32
F32R = mybir.dt.float32r
BF16 = mybir.dt.bfloat16
U8 = mybir.dt.uint8
AX_X = mybir.AxisListType.X

P = 128
B = 8
D = 512
C = D // P
H = 32
HG = 2
G = H // HG
NB = 4
HALF = B // 2
TOK = HALF * P
BLOCKS = G * NB
EPS = 1e-5
MASKED = 1e30
E, DK, R = 8, 32, 16
ER = E * R
QKA = 2 * E * DK + ER
HQ = QKA // 2
QK0, QK1, WV, WO = range(4)


def build(nc, x, ctx_t, mask, bias, ln_w, wq, wk, wv, wo, f_w, f_b, f_wq, f_wk, f_a, f_bm, out):
    with ExitStack() as ctx:
        def sb(name, shape, dt):
            return ctx.enter_context(nc.sbuf_tensor(name, shape, dt))

        def sem(name):
            return ctx.enter_context(nc.semaphore(name))

        x_hi = sb("x_hi", [P, C, B * P], F32R)
        x_lo = sb("x_lo", [P, C, B * P], F32R)
        c_hi = sb("c_hi", [P, C, B * P], F32R)
        c_lo = sb("c_lo", [P, C, B * P], F32R)
        resid = sb("resid", [P, B, D], F32)
        q_t = sb("q_t", [P, HG, B * P], F32)
        k_t = sb("k_t", [P, HG, B * P], F32)
        v_sb = sb("v_sb", [P, 2, B, HG * P], F32)
        at_hi = sb("at_hi", [P, HG, B * P], F32R)
        at_lo = sb("at_lo", [P, HG, B * P], F32R)
        raw = sb("raw", [P, 4, 1024], F32)
        wqk_hi = sb("wqk_hi", [P, HG, 2, C, P], F32R)
        wqk_lo = sb("wqk_lo", [P, HG, 2, C, P], F32R)
        wv_hi = sb("wv_hi", [P, 2, C, HG * P], F32R)
        wv_lo = sb("wv_lo", [P, 2, C, HG * P], F32R)
        wo_hi = sb("wo_hi", [P, 2, HG, D], F32R)
        wo_lo = sb("wo_lo", [P, 2, HG, D], F32R)
        bias_mask = sb("bias_mask", [P, 2, HALF, P], F32)
        mask_neg = sb("mask_neg", [P, B, P], BF16)
        bias_sb = sb("bias_sb", [P, 2, HG, P], F32)
        probs = sb("probs", [P, 2, HALF, P], F32)
        probs_t = sb("probs_t", [P, HALF * P], F32)
        ident = sb("ident", [P, P], F32)
        row_valid = sb("row_valid", [P, B], F32)
        neg_max = sb("neg_max", [P, 2, HALF], F32)
        row_sum = sb("row_sum", [P, 2, HALF], F32)
        row_inv = sb("row_inv", [P, 2, HALF], F32)
        ln_sb = sb("ln_sb", [P, C], F32)
        stats = sb("stats", [P, 6], F32)
        mean_var = sb("mean_var", [P, B, 2], F32)
        variances = sb("variances", [P, 2, B], F32)
        inv_root = sb("inv_root", [P, 2, B], F32)
        minus_half = sb("minus_half", [P, 2, B], F32)
        rstd, norm_rms = inv_root[:, 0], inv_root[:, 1]

        ctx_raw = [v_sb[:, 1].rearrange("p b n -> p (b n)").rearrange("p (c t) -> p c t", c=C),
                   q_t[:, :, :].rearrange("p h t -> p (h t)").rearrange("p (c t) -> p c t", c=C)]
        x_normed = v_sb[:, 1].rearrange("p b n -> p (b n)").rearrange("p (b d) -> p b d", b=HALF)
        mask_raw = probs_t[:, 0:B * P // 4].bitcast(U8)
        flat_v0 = v_sb[:, 0].rearrange("p b n -> p (b n)")
        flat_q = q_t[:, :, :].rearrange("p h t -> p (h t)")
        flat_k = k_t[:, :, :].rearrange("p h t -> p (h t)")
        fw_raw = raw[:, QK0:QK1 + 1].rearrange("p a n -> p (a n)").rearrange("p (c n) -> p c n", c=C)
        fq_raw = raw[:, WV].rearrange("p (c n) -> p c n", c=C)
        fk_raw = flat_v0[:, 0:1024].rearrange("p (c n) -> p c n", c=C)
        fa_raw = flat_v0[:, 1024:1536].rearrange("p (c n) -> p c n", c=C)
        bm_sb = flat_v0[:, 1536:2048]
        fb_sb = raw[:, WO, 0:D]
        y_sb = [flat_q[:, i * D:(i + 1) * D] for i in range(2)]
        resid_b = [flat_q[:, (2 + i) * D:(3 + i) * D] for i in range(2)]
        qka_sb = [flat_k[:, i * QKA:(i + 1) * QKA] for i in range(2)]
        prod = flat_k[:, 2 * QKA:2 * QKA + E * DK]
        at = 2 * QKA + E * DK
        u_sb = [flat_k[:, at + i * ER:at + (i + 1) * ER] for i in range(2)]
        u_t = [flat_k[:, at + (2 + i) * ER:at + (3 + i) * ER] for i in range(2)]
        router = sb("router", [P, 2, E], F32)
        router_e = sb("router_e", [P, 2, E], F32)
        router_nm = sb("router_nm", [P, 2], F32)
        router_sum = sb("router_sum", [P, 2], F32)
        router_inv = sb("router_inv", [P, 2], F32)

        def bank(name):
            return ctx.enter_context(nc.psum_tensor(name, [P, 512], F32))

        ps_q, ps_k, ps_v, ps_s, ps_pt, ps_pv, ps_o0, ps_o1 = [
            bank(n) for n in ("ps_q", "ps_k", "ps_v", "ps_s", "ps_pt", "ps_pv", "ps_o0", "ps_o1")]
        ps_o = (ps_o0, ps_o1)
        ps_x = (ps_o0, ps_o1, ps_s, ps_pt)
        ps_w = (ps_q, ps_k)
        ps_a = (ps_s, ps_pt)
        ps_yt, ps_ut = ps_v, ps_pv

        ctx_in = [sem(f"ctx_in{i}") for i in range(C + 1)]
        x_in = [sem(f"x_in{i}") for i in range(2)]
        small_in = sem("small_in")
        raw_in = [sem(f"raw_in{i}") for i in range(4)]
        k_raw_in = [sem(f"k_raw_in{i}") for i in range(HG)]
        bias_in = [sem("bias_in0"), sem("bias_in1")]
        ffn_in = sem("ffn_in")
        ffn_late_in = sem("ffn_late_in")
        bvec_in = sem("bvec_in")
        stored = sem("stored")
        w_hi_done = [sem(f"w_hi_done{i}") for i in range(4)]
        w_lo_done = [sem(f"w_lo_done{i}") for i in range(4)]
        k0_hi_done = sem("k0_hi_done")
        k0_lo_done = sem("k0_lo_done")
        f_hi_done = sem("f_hi_done")
        fw_lo_done = sem("fw_lo_done")
        f_lo_done = sem("f_lo_done")
        ident_zero = sem("ident_zero")
        consts_ready = sem("consts_ready")
        mask_ready = sem("mask_ready")
        c_hi_done = sem("c_hi_done")
        c_lo_done = sem("c_lo_done")
        stats_done = sem("stats_done")
        aggr_done = sem("aggr_done")
        var_done = sem("var_done")
        root_done = sem("root_done")
        hidden_done = sem("hidden_done")
        resid_done = sem("resid_done")
        normed_done = sem("normed_done")
        xt_done = sem("xt_done")
        x_hi_done = sem("x_hi_done")
        x_lo_done = sem("x_lo_done")
        q_done, k_done, v_done = sem("q_done"), sem("k_done"), sem("v_done")
        q_ready, k_ready, v_ready = sem("q_ready"), sem("k_ready"), sem("v_ready")
        bm_ready = sem("bm_ready")
        scores_done = sem("scores_done")
        scores_read = sem("scores_read")
        max_done = sem("max_done")
        exp_done = sem("exp_done")
        inv_done = sem("inv_done")
        probs_ready = sem("probs_ready")
        pt_done = sem("pt_done")
        pt_copied = sem("pt_copied")
        pv_done = sem("pv_done")
        at_hi_done = sem("at_hi_done")
        at_lo_done = sem("at_lo_done")
        o_done = sem("o_done")
        o_added = sem("o_added")
        f_stats, f_aggr, f_eps, f_rstd = sem("f_stats"), sem("f_aggr"), sem("f_eps"), sem("f_rstd")
        y_done, yt_done, yt_hi, yt_lo = sem("y_done"), sem("yt_done"), sem("yt_hi"), sem("yt_lo")
        resid_b_done = sem("resid_b_done")
        fa_done, fa_copied = sem("fa_done"), sem("fa_copied")
        prod_done, route_sum, route_scaled = sem("prod_done"), sem("route_sum"), sem("route_scaled")
        route_max, route_exp, route_inv = sem("route_max"), sem("route_exp"), sem("route_inv")
        u_done, ut_done, ut_copied = sem("u_done"), sem("ut_done"), sem("ut_copied")
        fo_done, result_done = sem("fo_done"), sem("result_done")

        def per_group(engine, step):
            step(0, 0)
            with engine.Fori(1, G - 4, 2) as g:
                step(g, 1)
                step(g + 1, 0)
            for g in range(G - 3, G):
                step(g, g % 2)

        def exists(group):
            return not isinstance(group, int) or group < G

        block = ctx.enter_context(nc.Block())

        @block.sync
        def _(sp):
            def load(kind, g):
                if kind in (QK0, QK1):
                    h = HG * g + kind
                    sp.dma_start(raw[:, kind, 0:512], wq[h]).then_inc(raw_in[kind], 16)
                    sp.dma_start(raw[:, kind, 512:1024], wk[h]).then_inc(k_raw_in[kind], 16)
                elif kind == WV:
                    sp.dma_start(raw[:, WV, :], wv[g]).then_inc(raw_in[WV], 16)
                else:
                    sp.dma_start(raw[:, WO, :], wo[g]).then_inc(raw_in[WO], 16)

            def load_bias(g, p):
                sp.dma_start(bias_sb[:, p], bias[g]).then_inc(bias_in[p], 16)

            def load_x(half):
                bs = slice(HALF * half, HALF * (half + 1))
                sp.dma_start(resid[:, bs, :], x[bs].rearrange("b p d -> p b d")).then_inc(x_in[half], 16)

            for c in range(C):
                sp.dma_start(ctx_raw[0][:, c, :], ctx_t[:, 0, c]).then_inc(ctx_in[c], 16)
                if c == 0:
                    sp.dma_start(raw[:, QK0, 512:1024], wk[0]).then_inc(k_raw_in[0], 16)
            load(WV, 0)
            sp.dma_start(raw[:, QK1, 512:1024], wk[1]).then_inc(k_raw_in[1], 16)
            load_x(0)
            sp.dma_start(ctx_raw[1], ctx_t[:, 1]).then_inc(ctx_in[C], 16)
            sp.dma_start(mask_raw, mask).then_inc(small_in, 16)
            sp.dma_start(ln_sb[:, :], ln_w).then_inc(small_in, 16)
            for h in range(HG):
                sp.dma_start(raw[:, QK0 + h, 0:512], wq[h]).then_inc(raw_in[QK0 + h], 16)
            load_x(1)
            load_bias(0, 0)
            load_bias(1, 1)
            sp.wait_ge(w_lo_done[WV], 1)
            load(WV, 1)
            sp.wait_ge(w_lo_done[QK0], 1)
            load(QK0, 1)
            sp.wait_ge(w_lo_done[QK1], 1)
            load(QK1, 1)
            load(WO, 0)
            sp.wait_ge(w_lo_done[WV], 2)
            load(WV, 2)
            sp.wait_ge(w_lo_done[QK0], 2)
            load(QK0, 2)

            def step(g, p):
                if exists(g + 2):
                    sp.wait_ge(w_lo_done[QK1], g + 2)
                    load(QK1, g + 2)
                if exists(g + 3):
                    sp.wait_ge(w_lo_done[WV], g + 3)
                    load(WV, g + 3)
                if exists(g + 1):
                    sp.wait_ge(w_lo_done[WO], g + 1)
                    load(WO, g + 1)
                if exists(g + 2):
                    sp.wait_ge(bm_ready, NB * g + NB)
                    load_bias(g + 2, p)
                if exists(g + 3):
                    sp.wait_ge(w_lo_done[QK0], g + 3)
                    load(QK0, g + 3)
                if isinstance(g, int) and g == G - 2:
                    sp.wait_ge(w_lo_done[QK0], G)
                    sp.wait_ge(w_lo_done[QK1], G)
                    sp.wait_ge(w_lo_done[WV], G)
                    sp.dma_start(fw_raw, f_w).then_inc(ffn_in, 16)
                    sp.dma_start(fq_raw, f_wq).then_inc(ffn_in, 16)
                    sp.wait_ge(pv_done, BLOCKS - NB)
                    sp.dma_start(fk_raw, f_wk).then_inc(ffn_late_in, 16)
                    sp.dma_start(fa_raw, f_a).then_inc(ffn_late_in, 16)
                    sp.dma_start(bm_sb, f_bm).then_inc(ffn_late_in, 16)
                if isinstance(g, int) and g == G - 1:
                    sp.wait_ge(w_lo_done[WO], G)
                    sp.dma_start(fb_sb, f_b.to_broadcast([P, D])).then_inc(bvec_in, 16)

            per_group(sp, step)
            for b in range(B):
                sp.wait_ge(result_done, b + 1)
                sp.dma_start(out[b], resid[:, b, :]).then_inc(stored, 16)
            sp.wait_ge(stored, 16 * B)

        @block.gpsimd
        def _(pool):
            nc.gpsimd.memset(ident[:, :], 0.0).then_inc(ident_zero, 1)
            pool.wait_ge(ident_zero, 1)
            nc.gpsimd.affine_select(out=ident[:, :], in_=ident[:, :], compare_op=ALU.not_equal, fill=1.0,
                                    base=0, pattern=[[-1, P]], channel_multiplier=1).then_inc(consts_ready, 1)
            nc.gpsimd.memset(minus_half[:, :, :], -0.5).then_inc(consts_ready, 1)
            pool.wait_ge(consts_ready, 2)
            for half in range(2):
                bs = slice(HALF * half, HALF * (half + 1))
                pool.wait_ge(var_done, 2 * (half + 1))
                nc.gpsimd.tensor_tensor(inv_root[:, :, bs], variances[:, :, bs], minus_half[:, :, bs],
                                        ALU.pow).then_inc(root_done, 1)
            pool.wait_ge(mask_ready, 1)

            def add_hidden(b):
                pool.wait_ge(hidden_done, b + 1)
                nc.gpsimd.tensor_tensor(resid[:, b, :], resid[:, b, :], x_normed[:, b % HALF, :],
                                        ALU.add).then_inc(resid_done, 1)

            def bias_and_mask(s, g, j, p):
                if not isinstance(s, int) or s >= 2:
                    pool.wait_ge(scores_read, s - 1)
                head, half = j % 2, j // 2
                one = bias_sb[:, p, head:head + 1, :].to_broadcast([P, HALF, P])
                nc.gpsimd.tensor_tensor(bias_mask[:, j % 2], one,
                                        mask_neg[:, HALF * half:HALF * (half + 1), :], ALU.add).then_inc(bm_ready, 1)

            def split_hi(r, hi):
                nc.gpsimd.tensor_copy(hi, r).then_inc(f_hi_done, 1)

            def step(g, p):
                if isinstance(g, int):
                    pool.wait_ge(bias_in[p], 16 * (g // 2 + 1))
                else:
                    pool.wait_ge(bias_in[p], 8 * (g - p) + 16)
                for j in range(NB):
                    bias_and_mask(NB * g + j, g, j, p)
                    if isinstance(g, int) and g == 0 and j == 1:
                        for b in range(B):
                            add_hidden(b)
                    if isinstance(g, int) and g == G - 1 and j == 1:
                        pool.wait_ge(v_done, BLOCKS)
                        pool.wait_ge(ffn_in, 16 * 2)
                        split_hi(fq_raw, c_hi[:, :, 0:E * DK])
                        split_hi(fw_raw, x_hi[:, :, 0:D])
                    if isinstance(g, int) and g == G - 1 and j == 2:
                        pool.wait_ge(ffn_late_in, 16 * 3)
                        split_hi(fk_raw, c_hi[:, :, E * DK:2 * E * DK])
                        split_hi(fa_raw, c_hi[:, :, 2 * E * DK:QKA])

            per_group(pool, step)
            pool.wait_ge(f_hi_done, 2)
            nc.gpsimd.tensor_tensor(x_lo[:, :, 0:D], fw_raw, x_hi[:, :, 0:D].bitcast(F32),
                                    ALU.subtract).then_inc(fw_lo_done, 1)
            pool.wait_ge(bvec_in, 16)

            def inverse_deviation(b):
                pool.wait_ge(f_eps, b + 1)
                nc.gpsimd.tensor_tensor(rstd[:, b:b + 1], variances[:, 0, b:b + 1], minus_half[:, 0, 0:1], ALU.pow).then_inc(f_rstd, 1)

            inverse_deviation(0)
            inverse_deviation(1)
            for b in range(B):
                if b >= 2:
                    pool.wait_ge(result_done, b - 1)
                nc.gpsimd.tensor_tensor(resid_b[b % 2], resid[:, b, :], fb_sb, ALU.add).then_inc(resid_b_done, 1)
                if b + 2 < B:
                    inverse_deviation(b + 2)

        def weight_parts(kind, p):
            def flat(t):
                names = " ".join("abcd"[:len(t.shape) - 1])
                return t.rearrange(f"p {names} -> p ({names})")
            if kind in (QK0, QK1):
                return raw[:, kind], flat(wqk_hi[:, kind]), flat(wqk_lo[:, kind])
            if kind == WV:
                return raw[:, WV], flat(wv_hi[:, p]), flat(wv_lo[:, p])
            return raw[:, WO], flat(wo_hi[:, p]), flat(wo_lo[:, p])

        def output_banks(n, last):
            return (ps_q, ps_k) if last and n % 2 else ps_o

        def slot_weights(j, g, p):
            return [(QK1, g + 1, 0), (WV, g + 2, p), (WO, g, p), (QK0, g + 2, 0)][j]

        @block.scalar
        def _(act):
            def copy(o, i):
                return nc.scalar.activation(o, i, ACT.Copy)

            def split_hi(kind, group, p):
                act.wait_ge(raw_in[kind], 16 * (group + 1))
                if kind in (QK0, QK1):
                    act.wait_ge(k_raw_in[kind], 16 * (group + 1))
                r, hi, _ = weight_parts(kind, p)
                copy(hi, r).then_inc(w_hi_done[kind], 1)

            def q_out(n, j, bank=ps_q):
                act.wait_ge(q_done, n + 1)
                copy(q_t[:, j % 2, TOK * (j // 2):TOK * (j // 2 + 1)], bank[:, :]).then_inc(q_ready, 1)

            def k_out(n, j):
                act.wait_ge(k_done, n + 1)
                copy(k_t[:, j % 2, TOK * (j // 2):TOK * (j // 2 + 1)], ps_k[:, :]).then_inc(k_ready, 1)

            def v_out(n, j, p):
                act.wait_ge(v_done, n + 1)
                copy(v_sb[:, p, 2 * j:2 * j + 2, :].rearrange("p b n -> p (b n)"), ps_v[:, :]).then_inc(v_ready, 1)

            def x_high(n):
                half, c = n // C, n % C
                act.wait_ge(xt_done, n + 1)
                nc.scalar.activation(x_hi[:, c, TOK * half:TOK * (half + 1)], ps_x[c][:, :], ACT.Copy,
                                     scale=ln_sb[:, c:c + 1]).then_inc(x_hi_done, 1)

            def k0_hi(h):
                act.wait_ge(k_raw_in[h], 16)
                copy(wqk_hi[:, h, 1].rearrange("p c n -> p (c n)"), raw[:, QK0 + h, 512:1024]).then_inc(k0_hi_done, 1)

            def q0_hi(h):
                act.wait_ge(raw_in[QK0 + h], 16)
                copy(wqk_hi[:, h, 0].rearrange("p c n -> p (c n)"), raw[:, QK0 + h, 0:512]).then_inc(w_hi_done[h], 1)

            for c in range(C):
                act.wait_ge(ctx_in[c], 16)
                copy(c_hi[:, c, 0:TOK], ctx_raw[0][:, c, :]).then_inc(c_hi_done, 1)
                if c == 0:
                    k0_hi(0)
            split_hi(WV, 0, 0)
            k0_hi(1)
            k_out(0, 0)
            v_out(0, 0, 0)
            act.wait_ge(ctx_in[C], 16)
            copy(c_hi[:, :, TOK:2 * TOK], ctx_raw[1]).then_inc(c_hi_done, 1)
            k_out(1, 1)
            v_out(1, 1, 0)
            for h in range(HG):
                q0_hi(h)
            k_out(2, 2)
            act.wait_ge(small_in, 32)
            for n in range(C):
                x_high(n)
            v_out(2, 2, 0)
            k_out(3, 3)
            q_out(0, 0)
            split_hi(WV, 1, 1)
            v_out(3, 3, 0)
            for n in range(C, 2 * C):
                x_high(n)
            q_out(1, 1)
            q_out(2, 2, ps_o0)
            split_hi(QK0, 1, 0)
            q_out(3, 3)

            def step(g, p):
                s0 = NB * g
                last = isinstance(g, int) and g == G - 1
                for j in range(NB):
                    s = s0 + j
                    kind, group, wp = slot_weights(j, g, p)
                    if exists(group):
                        if kind in (QK0, QK1):
                            act.wait_ge(k_done, s + 4)
                        elif kind == WV:
                            act.wait_ge(v_done, s + 3)
                        elif not isinstance(g, int) or g >= 2:
                            act.wait_ge(o_done, s - 6)
                        split_hi(kind, group, wp)
                    if last:
                        probs_out(s)
                    act.wait_ge(max_done, s + 1)
                    for i in range(HALF):
                        e = nc.scalar.activation(probs[:, j % 2, i, :], probs[:, j % 2, i, :], ACT.Exp,
                                                 bias=neg_max[:, j % 2, i:i + 1],
                                                 accum_out=row_sum[:, j % 2, i:i + 1])
                    e.then_inc(exp_done, 1)
                    if not last and (j > 0 or not isinstance(g, int) or g > 0):
                        probs_out(s)
                    if not last:
                        q_out(s + NB, j)
                        k_out(s + NB, j)
                    if j > 0 or not isinstance(g, int) or g > 0:
                        at_high(s, j)
                    if not last:
                        if isinstance(g, int) and g == 0 and j == 0:
                            act.wait_ge(resid_done, B)
                        v_out(s + NB, j, 1 - p)

            def probs_out(s):
                act.wait_ge(pt_done, s)
                copy(probs_t[:, :], ps_pt[:, :]).then_inc(pt_copied, 1)

            def at_high(s, j):
                jj = (j - 1) % NB
                act.wait_ge(pv_done, s)
                copy(at_hi[:, jj % 2, TOK * (jj // 2):TOK * (jj // 2 + 1)], ps_pv[:, :]).then_inc(at_hi_done, 1)

            per_group(act, step)
            probs_out(BLOCKS)
            at_high(BLOCKS, 0)

            def yt_high(b):
                act.wait_ge(yt_done, b + 1)
                copy(x_hi[:, :, D + P * (b % 2):D + P * (b % 2 + 1)],
                     ps_yt[:, :].rearrange("p (c t) -> p c t", c=C)).then_inc(yt_hi, 1)

            yt_high(0)
            yt_high(1)
            for b in range(B):
                act.wait_ge(fa_done, b + 1)
                if b >= 2:
                    act.wait_ge(u_done, b - 1)
                for i in range(2):
                    a = copy(qka_sb[b % 2][:, HQ * i:HQ * (i + 1)], ps_a[i][:, 0:HQ])
                a.then_inc(fa_copied, 1)
                act.wait_ge(route_max, b + 1)
                nc.scalar.activation(router_e[:, b % 2, :], router[:, b % 2, :], ACT.Exp,
                                     bias=router_nm[:, b % 2:b % 2 + 1],
                                     accum_out=router_sum[:, b % 2:b % 2 + 1]).then_inc(route_exp, 1)
                if b + 2 < B:
                    yt_high(b + 2)
                act.wait_ge(ut_done, b + 1)
                copy(u_t[b % 2], ps_ut[:, 0:P]).then_inc(ut_copied, 1)

        @block.vector
        def _(dve):
            def sub(o, a, hi):
                return nc.vector.tensor_tensor(o, a, hi.bitcast(F32), ALU.subtract)

            def split_lo(kind, group, p):
                dve.wait_ge(w_hi_done[kind], group + 1)
                r, hi, lo = weight_parts(kind, p)
                sub(lo, r, hi).then_inc(w_lo_done[kind], 1)

            def tile_stats(b, n, done, aggregated):
                if n > 0:
                    dve.wait_ge(aggregated, n)
                nc.vector.bn_stats(stats[:, :], resid[:, b, :]).then_inc(done, 1)
                dve.wait_ge(done, n + 1)
                nc.vector.bn_aggr(mean_var[:, b, :], stats[:, :]).then_inc(aggregated, 1)

            def x_low(n):
                half, c = n // C, n % C
                ts = slice(TOK * half, TOK * (half + 1))
                dve.wait_ge(x_hi_done, n + 1)
                nc.vector.scalar_tensor_tensor(out=x_lo[:, c, ts], in0=ps_x[c][:, :], scalar=ln_sb[:, c:c + 1],
                                               in1=x_hi[:, c, ts].bitcast(F32), op0=ALU.mult,
                                               op1=ALU.subtract).then_inc(x_lo_done, 1)

            def c_low(n, c, ts, src):
                dve.wait_ge(c_hi_done, n)
                sub(c_lo[:, c, ts], src, c_hi[:, c, ts]).then_inc(c_lo_done, 1)

            def k0_lo(h):
                dve.wait_ge(k0_hi_done, h + 1)
                sub(wqk_lo[:, h, 1].rearrange("p c n -> p (c n)"), raw[:, QK0 + h, 512:1024],
                    wqk_hi[:, h, 1].rearrange("p c n -> p (c n)")).then_inc(k0_lo_done, 1)

            def q0_lo(h):
                dve.wait_ge(w_hi_done[h], 1)
                sub(wqk_lo[:, h, 0].rearrange("p c n -> p (c n)"), raw[:, QK0 + h, 0:512],
                    wqk_hi[:, h, 0].rearrange("p c n -> p (c n)")).then_inc(w_lo_done[h], 1)

            def half_stats(half):
                bs = slice(HALF * half, HALF * (half + 1))
                dve.wait_ge(x_in[half], 16)
                for b in range(HALF * half, HALF * (half + 1)):
                    tile_stats(b, b, stats_done, aggr_done)
                dve.wait_ge(aggr_done, HALF * (half + 1))
                nc.vector.tensor_scalar(variances[:, 0, bs], mean_var[:, bs, 1], EPS, None, ALU.add).then_inc(var_done, 1)
                nc.vector.tensor_scalar(variances[:, 1, bs], mean_var[:, bs, 1], 1.0 + EPS, EPS * EPS,
                                        ALU.mult, ALU.add).then_inc(var_done, 1)

            def half_normed(half):
                dve.wait_ge(root_done, half + 1)
                if half == 0:
                    dve.wait_ge(c_lo_done, C)
                else:
                    dve.wait_ge(xt_done, C)
                for b in range(HALF * half, HALF * (half + 1)):
                    nc.vector.tensor_scalar(x_normed[:, b % HALF, :], resid[:, b, :], mean_var[:, b, 0:1],
                                            norm_rms[:, b:b + 1], ALU.subtract, ALU.mult).then_inc(normed_done, 1)

            def hidden(b):
                if b >= HALF:
                    dve.wait_ge(resid_done, b - HALF + 1)
                nc.vector.tensor_scalar(x_normed[:, b % HALF, :], resid[:, b, :], mean_var[:, b, 0:1],
                                        rstd[:, b:b + 1], ALU.subtract, ALU.mult).then_inc(hidden_done, 1)

            for c in range(C):
                c_low(c + 1, c, slice(0, TOK), ctx_raw[0][:, c, :])
                if c == 0:
                    k0_lo(0)
            split_lo(WV, 0, 0)
            k0_lo(1)
            half_stats(0)
            dve.wait_ge(small_in, 32)
            nc.vector.tensor_scalar(mask_neg[:, :, :].rearrange("p b k -> p (b k)"), mask_raw, -1.0, MASKED,
                                    ALU.add, ALU.mult).then_inc(mask_ready, 1)
            c_low(C + 1, slice(0, C), slice(TOK, 2 * TOK), ctx_raw[1])
            half_normed(0)
            for h in range(HG):
                q0_lo(h)
            for n in range(C):
                x_low(n)
            half_stats(1)
            nc.vector.tensor_reduce(row_valid[:, :], mask_raw.rearrange("p (b k) -> p b k", b=B),
                                    AX_X, ALU.max).then_inc(mask_ready, 1)
            half_normed(1)
            split_lo(WV, 1, 1)
            for n in range(C, 2 * C):
                x_low(n)
            dve.wait_ge(xt_done, 2 * C)
            for b in range(HALF):
                hidden(b)
            split_lo(QK0, 1, 0)
            for b in range(HALF, B):
                hidden(b)
            dve.wait_ge(mask_ready, 2)

            def add_output(n, j, last=False):
                dve.wait_ge(o_done, n + 1)
                for i in range(2):
                    a = nc.vector.tensor_tensor(resid[:, 2 * j + i, :], output_banks(n, last)[i][:, :], resid[:, 2 * j + i, :], ALU.add)
                a.then_inc(o_added, 1)

            def at_low(s, j):
                jj = (j - 1) % NB
                ts = slice(TOK * (jj // 2), TOK * (jj // 2 + 1))
                dve.wait_ge(at_hi_done, s)
                sub(at_lo[:, jj % 2, ts], ps_pv[:, :], at_hi[:, jj % 2, ts]).then_inc(at_lo_done, 1)

            def step(g, p):
                later = not isinstance(g, int) or g > 0
                for j in range(NB):
                    s = NB * g + j
                    half = j // 2
                    pr = probs[:, j % 2]
                    dve.wait_ge(scores_done, s + 1)
                    dve.wait_ge(bm_ready, s + 1)
                    nc.vector.tensor_tensor(pr, ps_s[:, :].rearrange("p (b k) -> p b k", b=HALF),
                                            bias_mask[:, j % 2], ALU.add).then_inc(scores_read, 1)
                    dve.wait_ge(scores_read, s + 1)
                    nc.vector.tensor_reduce(neg_max[:, j % 2, :], pr, AX_X, ALU.max, negate=True).then_inc(max_done, 1)
                    if later:
                        add_output(s - 4, j, isinstance(g, int) and g == G - 1 and j > 0)
                    kind, group, wp = slot_weights(j, g, p)
                    if exists(group):
                        split_lo(kind, group, wp)
                    if isinstance(g, int) and g == G - 1 and j > 0:
                        r, ns = [(fq_raw, slice(0, E * DK)), (fk_raw, slice(E * DK, 2 * E * DK)),
                                 (fa_raw, slice(2 * E * DK, QKA))][j - 1]
                        dve.wait_ge(f_hi_done, (1, 3, 4)[j - 1])
                        sub(c_lo[:, :, ns], r, c_hi[:, :, ns]).then_inc(f_lo_done, 1)
                    dve.wait_ge(exp_done, s + 1)
                    nc.vector.reciprocal(row_inv[:, j % 2, :], row_sum[:, j % 2, :]).then_inc(inv_done, 1)
                    dve.wait_ge(inv_done, s + 1)
                    for i in range(HALF):
                        b = HALF * half + i
                        n = nc.vector.tensor_scalar(pr[:, i, :], pr[:, i, :], row_inv[:, j % 2, i:i + 1],
                                                    row_valid[:, b:b + 1], ALU.mult, ALU.mult)
                    n.then_inc(probs_ready, 1)
                    if later or j > 0:
                        at_low(s, j)
                    if isinstance(g, int) and g == 0 and j == NB - 1:
                        dve.wait_ge(resid_done, B)

            per_group(dve, step)

            def normalise(b):
                tile_stats(b, b, f_stats, f_aggr)
                dve.wait_ge(f_aggr, b + 1)
                nc.vector.tensor_scalar(variances[:, 0, b:b + 1], mean_var[:, b, 1:2], EPS, None, ALU.add).then_inc(f_eps, 1)

            def normalised(b):
                dve.wait_ge(f_rstd, b + 1)
                if b >= 2:
                    dve.wait_ge(yt_done, b - 1)
                nc.vector.tensor_scalar(y_sb[b % 2], resid[:, b, :], mean_var[:, b, 0:1], rstd[:, b:b + 1],
                                        ALU.subtract, ALU.mult).then_inc(y_done, 1)

            def yt_low(b):
                ts = slice(D + P * (b % 2), D + P * (b % 2 + 1))
                dve.wait_ge(yt_hi, b + 1)
                sub(x_lo[:, :, ts], ps_yt[:, :].rearrange("p (c t) -> p c t", c=C), x_hi[:, :, ts]).then_inc(yt_lo, 1)

            def result(b):
                dve.wait_ge(fo_done, b + 1)
                dve.wait_ge(resid_b_done, b + 1)
                nc.vector.tensor_tensor(resid[:, b, :], ps_w[b % 2][:, :], resid_b[b % 2],
                                        ALU.add).then_inc(result_done, 1)

            add_output(BLOCKS - 4, 0, True)
            dve.wait_ge(o_added, BLOCKS - 3)
            normalise(0)
            normalised(0)
            at_low(BLOCKS, 0)
            add_output(BLOCKS - 3, 1, True)
            dve.wait_ge(o_added, BLOCKS - 2)
            normalise(1)
            yt_low(0)
            normalised(1)
            add_output(BLOCKS - 2, 2, True)
            add_output(BLOCKS - 1, 3, True)
            dve.wait_ge(o_added, BLOCKS)
            for b in range(B):
                if b + 1 < B:
                    yt_low(b + 1)
                if b + 2 < B:
                    normalise(b + 2)
                    normalised(b + 2)
                q = b % 2
                dve.wait_ge(fa_copied, b + 1)
                nc.vector.tensor_tensor(prod, qka_sb[q][:, 0:E * DK], qka_sb[q][:, E * DK:2 * E * DK],
                                        ALU.mult).then_inc(prod_done, 1)
                dve.wait_ge(prod_done, b + 1)
                nc.vector.tensor_reduce(router[:, q, :], prod.rearrange("p (e d) -> p e d", e=E),
                                        AX_X, ALU.add).then_inc(route_sum, 1)
                dve.wait_ge(route_sum, b + 1)
                nc.vector.tensor_scalar(router[:, q, :], router[:, q, :], float(DK) ** -0.5, None,
                                        ALU.mult).then_inc(route_scaled, 1)
                dve.wait_ge(route_scaled, b + 1)
                nc.vector.tensor_reduce(router_nm[:, q:q + 1], router[:, q, :], AX_X, ALU.max,
                                        negate=True).then_inc(route_max, 1)
                dve.wait_ge(route_exp, b + 1)
                nc.vector.reciprocal(router_inv[:, q:q + 1], router_sum[:, q:q + 1]).then_inc(route_inv, 1)
                dve.wait_ge(route_inv, b + 1)
                nc.vector.scalar_tensor_tensor(
                    out=u_sb[q].rearrange("p (e r) -> p e r", e=E),
                    in0=qka_sb[q][:, 2 * E * DK:QKA].rearrange("p (e r) -> p e r", e=E),
                    scalar=router_inv[:, q:q + 1],
                    in1=router_e[:, q, :].rearrange("p (e o) -> p e o", o=1).to_broadcast([P, E, R]),
                    op0=ALU.mult, op1=ALU.mult).then_inc(u_done, 1)
                if b > 0:
                    result(b - 1)
            result(B - 1)

        @block.tensor
        def _(pe):
            def passes(o, terms):
                for n, (lh, ll, rh, rl) in enumerate(terms):
                    pe.matmul(o, lh, rh, start=(n == 0), stop=False)
                    pe.matmul(o, lh, rl, start=False, stop=False)
                    m = pe.matmul(o, ll, rh, start=False, stop=(n == len(terms) - 1))
                return m

            def project(o, which, head, a_hi, a_lo, half):
                ts = slice(TOK * half, TOK * (half + 1))
                return passes(o, [(wqk_hi[:, head, which, c, :], wqk_lo[:, head, which, c, :],
                                   a_hi[:, c, ts], a_lo[:, c, ts]) for c in range(C)])

            def q_block(n, j, weights, into=ps_q):
                if j < 2:
                    pe.wait_ge(w_lo_done[QK0 + j % 2], weights)
                if isinstance(n, int) and n == 3:
                    pe.wait_ge(q_ready, 2)
                elif not isinstance(n, int) or n > 0:
                    pe.wait_ge(q_ready, n)
                project(into[:, :], 0, j % 2, x_hi, x_lo, j // 2).then_inc(q_done, 1)

            def k_block(n, j):
                if not isinstance(n, int) or n > 0:
                    pe.wait_ge(k_ready, n)
                project(ps_k[:, :], 1, j % 2, c_hi, c_lo, j // 2).then_inc(k_done, 1)

            def first_k_block():
                pe.wait_ge(k0_lo_done, 1)
                ts = slice(0, TOK)
                for c in range(C):
                    pe.wait_ge(c_lo_done, c + 1)
                    hi, lo = wqk_hi[:, 0, 1, c, :], wqk_lo[:, 0, 1, c, :]
                    pe.matmul(ps_k[:, :], hi, c_hi[:, c, ts], start=(c == 0), stop=False)
                    pe.matmul(ps_k[:, :], hi, c_lo[:, c, ts], start=False, stop=False)
                    m = pe.matmul(ps_k[:, :], lo, c_hi[:, c, ts], start=False, stop=(c == C - 1))
                m.then_inc(k_done, 1)

            def v_block(n, j, p, weights):
                if j == 0:
                    pe.wait_ge(w_lo_done[WV], weights)
                if not isinstance(n, int) or n > 0:
                    pe.wait_ge(v_ready, n)
                for i in range(2):
                    ts = slice(P * (2 * j + i), P * (2 * j + i + 1))
                    m = passes(ps_v[:, HG * P * i:HG * P * (i + 1)],
                               [(c_hi[:, c, ts], c_lo[:, c, ts], wv_hi[:, p, c, :], wv_lo[:, p, c, :])
                                for c in range(C)])
                m.then_inc(v_done, 1)

            def x_transposes(half):
                pe.wait_ge(normed_done, HALF * (half + 1))
                for c in range(C):
                    if half > 0:
                        pe.wait_ge(x_lo_done, c + 1)
                    for i in range(HALF):
                        m = pe.transpose(ps_x[c][:, P * i:P * (i + 1)], x_normed[:, i, P * c:P * (c + 1)],
                                         ident[:, :])
                    m.then_inc(xt_done, 1)

            def scores(s, j):
                head, half = j % 2, j // 2
                pe.wait_ge(q_ready, s + 1)
                pe.wait_ge(k_ready, s + 1)
                if not isinstance(s, int) or s > 0:
                    pe.wait_ge(scores_read, s)
                for i in range(HALF):
                    ts = slice(TOK * half + P * i, TOK * half + P * (i + 1))
                    m = pe.matmul(ps_s[:, P * i:P * (i + 1)], q_t[:, head, ts], k_t[:, head, ts],
                                  start=True, stop=True)
                m.then_inc(scores_done, 1)

            pe.wait_ge(consts_ready, 2)
            first_k_block()
            v_block(0, 0, 0, 1)
            pe.wait_ge(k0_lo_done, 2)
            k_block(1, 1)
            v_block(1, 1, 0, 1)
            pe.wait_ge(c_lo_done, C + 1)
            k_block(2, 2)
            x_transposes(0)
            v_block(2, 2, 0, 1)
            k_block(3, 3)
            pe.wait_ge(x_lo_done, C)
            q_block(0, 0, 1)
            v_block(3, 3, 0, 1)
            x_transposes(1)
            q_block(1, 1, 1)
            pe.wait_ge(x_lo_done, 2 * C)
            q_block(2, 2, 1, ps_o0)
            q_block(3, 3, 1)
            scores(0, 0)

            def turn_probs(s, j):
                pe.wait_ge(probs_ready, s)
                if not isinstance(s, int) or s > 1:
                    pe.wait_ge(pt_copied, s - 1)
                for i in range(HALF):
                    m = pe.transpose(ps_pt[:, P * i:P * (i + 1)], probs[:, (j - 1) % 2, i, :], ident[:, :])
                m.then_inc(pt_done, 1)

            def probs_v(s, j, p):
                jj = (j - 1) % NB
                vp = p if j > 0 else 1 - p
                pe.wait_ge(pt_copied, s)
                pe.wait_ge(v_ready, s - jj + 1 + 2 * (jj // 2))
                if not isinstance(s, int) or s > 1:
                    pe.wait_ge(at_lo_done, s - 1)
                for i in range(HALF):
                    m = pe.matmul(ps_pv[:, P * i:P * (i + 1)],
                                  v_sb[:, vp, HALF * (jj // 2) + i, P * (jj % 2):P * (jj % 2 + 1)],
                                  probs_t[:, P * i:P * (i + 1)], start=True, stop=True)
                m.then_inc(pv_done, 1)

            def output_pair(n, j, p, weights=0, last=False):
                nj = (j + 1) % NB
                wp = p if j == 3 else 1 - p
                if nj == 0:
                    pe.wait_ge(w_lo_done[WO], weights)
                pe.wait_ge(at_lo_done, n - nj + 2 + 2 * (nj // 2))
                if last and n == BLOCKS - 7:
                    pe.wait_ge(q_ready, BLOCKS)
                    pe.wait_ge(k_ready, BLOCKS)
                elif last:
                    pe.wait_ge(o_added, n - 1)
                elif not isinstance(n, int) or n > 0:
                    pe.wait_ge(o_added, n)
                banks = output_banks(n, last)
                for i in range(2):
                    ts = slice(P * (2 * nj + i), P * (2 * nj + i + 1))
                    m = passes(banks[i][:, :], [(at_hi[:, h, ts], at_lo[:, h, ts], wo_hi[:, wp, h, :],
                                                wo_lo[:, wp, h, :]) for h in range(HG)])
                m.then_inc(o_done, 1)

            def step(g, p):
                first = isinstance(g, int) and g == 0
                last = isinstance(g, int) and g == G - 1
                for j in range(NB):
                    s = NB * g + j
                    if not first or j > 0:
                        scores(s, j)
                    if not last:
                        q_block(s + NB, j, g + 2)
                    if not first or j > 0:
                        turn_probs(s, j)
                    if not last:
                        k_block(s + NB, j)
                    if last:
                        output_pair(s - 3, j, p, g + 1, True)
                    if not first or j > 0:
                        probs_v(s, j, p)
                    if not last:
                        v_block(s + NB, j, 1 - p, g + 2)
                    if not last and (not first or j == 3):
                        output_pair(s - 3, j, p, g + 1)

            per_group(pe, step)
            turn_probs(BLOCKS, 0)
            output_pair(BLOCKS - 3, 0, 0, last=True)
            probs_v(BLOCKS, 0, 0)

            def y_transposes(b):
                pe.wait_ge(y_done, b + 1)
                if b > 0:
                    pe.wait_ge(yt_lo, b)
                for c in range(C):
                    m = pe.transpose(ps_yt[:, P * c:P * (c + 1)], y_sb[b % 2][:, P * c:P * (c + 1)], ident[:, :])
                m.then_inc(yt_done, 1)

            def yt(b):
                ts = slice(D + P * (b % 2), D + P * (b % 2 + 1))
                return [(x_hi[:, c, ts], x_lo[:, c, ts]) for c in range(C)]

            y_transposes(0)
            output_pair(BLOCKS - 2, 1, 0, last=True)
            output_pair(BLOCKS - 1, 2, 0, last=True)
            y_transposes(1)
            pe.wait_ge(f_lo_done, 3)
            pe.wait_ge(fw_lo_done, 1)
            for b in range(B):
                pe.wait_ge(yt_lo, b + 1)
                if b > 0:
                    pe.wait_ge(fa_copied, b)
                for i in range(2):
                    ns = slice(HQ * i, HQ * (i + 1))
                    m = passes(ps_a[i][:, 0:HQ], [(*yt(b)[c], c_hi[:, c, ns], c_lo[:, c, ns]) for c in range(C)])
                m.then_inc(fa_done, 1)
                if b > 0:
                    pe.wait_ge(u_done, b)
                    pe.transpose(ps_ut[:, 0:P], u_sb[(b - 1) % 2], ident[:, :]).then_inc(ut_done, 1)
                if b >= 2:
                    pe.wait_ge(result_done, b - 1)
                elif b == 0:
                    pe.wait_ge(o_added, BLOCKS)
                for c in range(C):
                    yh, yl = yt(b)[c]
                    pe.matmul(ps_w[b % 2][:, :], yh, x_hi[:, c, 0:D], start=(c == 0), stop=False)
                    pe.matmul(ps_w[b % 2][:, :], yh, x_lo[:, c, 0:D], start=False, stop=False)
                    pe.matmul(ps_w[b % 2][:, :], yl, x_hi[:, c, 0:D], start=False, stop=False)
                if b > 0:
                    pe.wait_ge(ut_copied, b)
                    pe.matmul(ps_w[(b - 1) % 2][:, :], u_t[(b - 1) % 2], bm_sb, start=False,
                              stop=True).then_inc(fo_done, 1)
                if b + 2 < B:
                    y_transposes(b + 2)
            b = B - 1
            pe.wait_ge(u_done, b + 1)
            pe.transpose(ps_ut[:, 0:P], u_sb[b % 2], ident[:, :]).then_inc(ut_done, 1)
            pe.wait_ge(ut_copied, b + 1)
            pe.matmul(ps_w[b % 2][:, :], u_t[b % 2], bm_sb, start=False, stop=True).then_inc(fo_done, 1)


def kernel(x, ctx_4096, mask_BxSxS2_bk0, L0_xattn_position_bias, L0_xattn_ln_weight, L0_xattn_w_q,
           L0_xattn_w_k, L0_xattn_w_v, L0_xattn_w_out, L0_ffn_W, L0_ffn_b, L0_ffn_Wq, L0_ffn_Wk,
           L0_ffn_A, L0_ffn_Bm):
    import numpy as np
    import concourse.bacc as bacc
    from concourse.bass_utils import run_bass_kernel_spmd

    def heads(w):
        return np.asarray(w).reshape(H, P, C, P).transpose(0, 3, 2, 1).reshape(H, P, C * P)

    def turned(w):
        w = np.asarray(w)
        return w.reshape(w.shape[0], C, P).transpose(2, 1, 0)

    laid = {
        "x": np.asarray(x),
        "ctx_t": np.asarray(ctx_4096).reshape(2, TOK, C, P).transpose(3, 0, 2, 1),
        "mask": np.asarray(mask_BxSxS2_bk0).transpose(1, 0, 2).reshape(P, B * P),
        "bias": np.asarray(L0_xattn_position_bias).reshape(G, HG, P, P).transpose(0, 2, 1, 3),
        "ln_w": np.asarray(L0_xattn_ln_weight).reshape(C, P).T,
        "wq": heads(L0_xattn_w_q),
        "wk": heads(L0_xattn_w_k),
        "wv": np.asarray(L0_xattn_w_v).reshape(G, HG * P, C, P).transpose(0, 3, 2, 1).reshape(G, P, C * HG * P),
        "wo": np.asarray(L0_xattn_w_out).reshape(D, G, HG, P).transpose(1, 3, 2, 0).reshape(G, P, HG * D),
        "f_w": turned(L0_ffn_W),
        "f_b": np.asarray(L0_ffn_b).reshape(1, D),
        "f_wq": turned(L0_ffn_Wq),
        "f_wk": turned(L0_ffn_Wk),
        "f_a": turned(np.asarray(L0_ffn_A).reshape(ER, D)),
        "f_bm": np.asarray(L0_ffn_Bm).transpose(0, 2, 1).reshape(ER, D),
    }
    nc = bacc.Bacc("TRN2", target_bir_lowering=False, num_devices=1)
    arrays, args = {}, []
    for name, a in laid.items():
        a = np.ascontiguousarray(a)
        arrays[name] = a
        args.append(nc.dram_tensor(name, a.shape, mybir.dt.from_np(a.dtype), kind="ExternalInput").ap())
    result = nc.dram_tensor("out", (B, P, D), F32, kind="ExternalOutput").ap()
    build(nc, *args, result)
    r = run_bass_kernel_spmd(nc, [arrays], core_ids=[0])
    return r.results[0]["out"]
```

```python
from contextlib import ExitStack

import concourse.bass as bass
from concourse import mybir

ALU = mybir.AluOpType
ACT = mybir.ActivationFunctionType
F32 = mybir.dt.float32
F32R = mybir.dt.float32r
BF16 = mybir.dt.bfloat16
U8 = mybir.dt.uint8
AX_X = mybir.AxisListType.X

P = 128
B = 8
D = 512
C = D // P
H = 32
HG = 2
G = H // HG
NB = 4
SQUARE = 32
HALF = B // 2
TOK = HALF * P
BLOCKS = G * NB
EPS = 1e-5
MASKED = 1e30
E, DK, R = 8, 32, 16
ER = E * R
QKA = 2 * E * DK + ER
KA = QKA - E * DK
QK0, QK1, WV, WO = range(4)


def build(nc, x, ctx_t, mask, bias, ln_w, wq, wk, wv, wo, f_w, f_b, f_wq, f_wk, f_a, f_bm, out):
    with ExitStack() as ctx:
        def sb(name, shape, dt):
            return ctx.enter_context(nc.sbuf_tensor(name, shape, dt))

        def sem(name):
            return ctx.enter_context(nc.semaphore(name))

        x_hi = sb("x_hi", [P, C, B * P], F32R)
        x_lo = sb("x_lo", [P, C, B * P], F32R)
        c_hi = sb("c_hi", [P, C, B * P], F32R)
        c_lo = sb("c_lo", [P, C, B * P], F32R)
        resid = sb("resid", [P, B, D], F32)
        q_t = sb("q_t", [P, HG, B * P], F32)
        k_t = sb("k_t", [P, HG, B * P], F32)
        v_sb = sb("v_sb", [P, 2, B, HG * P], F32)
        at_hi = sb("at_hi", [P, HG, B * P], F32R)
        at_lo = sb("at_lo", [P, HG, B * P], F32R)
        raw = sb("raw", [P, 4, 1024], F32)
        wqk_hi = sb("wqk_hi", [P, HG, 2, C, P], F32R)
        wqk_lo = sb("wqk_lo", [P, HG, 2, C, P], F32R)
        wv_hi = sb("wv_hi", [P, 2, C, HG * P], F32R)
        wv_lo = sb("wv_lo", [P, 2, C, HG * P], F32R)
        wo_hi = sb("wo_hi", [P, 2, HG, D], F32R)
        wo_lo = sb("wo_lo", [P, 2, HG, D], F32R)
        bias_mask = sb("bias_mask", [P, 2, HALF, P], F32)
        mask_neg = sb("mask_neg", [P, B, P], BF16)
        bias_sb = sb("bias_sb", [P, 2, HG, P], F32)
        probs = sb("probs", [P, 2, HALF, P], F32)
        probs_t = sb("probs_t", [P, HALF * P], F32)
        ident = sb("ident", [P, P], F32)
        row_valid = sb("row_valid", [P, B], F32)
        neg_max = sb("neg_max", [P, 2, HALF], F32)
        row_sum = sb("row_sum", [P, 2, HALF], F32)
        row_inv = sb("row_inv", [P, 2, HALF], F32)
        ln_sb = sb("ln_sb", [P, C], F32)
        stats = sb("stats", [P, 6], F32)
        mean_var = sb("mean_var", [P, B, 2], F32)
        variances = sb("variances", [P, 2, B], F32)
        inv_root = sb("inv_root", [P, 2, B], F32)
        minus_half = sb("minus_half", [P, 2, B], F32)
        rstd, norm_rms = inv_root[:, 0], inv_root[:, 1]

        ctx_raw = [v_sb[:, 1].rearrange("p b n -> p (b n)").rearrange("p (c t) -> p c t", c=C),
                   q_t[:, :, :].rearrange("p h t -> p (h t)").rearrange("p (c t) -> p c t", c=C)]
        x_normed = v_sb[:, 1].rearrange("p b n -> p (b n)").rearrange("p (b d) -> p b d", b=HALF)
        mask_raw = probs_t[:, 0:B * P // 4].bitcast(U8)
        flat_v0 = v_sb[:, 0].rearrange("p b n -> p (b n)")
        flat_q = q_t[:, :, :].rearrange("p h t -> p (h t)")
        flat_k = k_t[:, :, :].rearrange("p h t -> p (h t)")
        fw_raw = raw[:, QK0:QK1 + 1].rearrange("p a n -> p (a n)").rearrange("p (c n) -> p c n", c=C)
        fq_raw = raw[:, WV].rearrange("p (c n) -> p c n", c=C)
        fw_hi, fw_lo = x_hi[:, :, 0:D], x_lo[:, :, 0:D]
        fq_hi, fq_lo = wv_hi[:, 0], wv_lo[:, 0]
        fka_hi, fka_lo = c_hi[:, :, 0:KA], c_lo[:, :, 0:KA]
        fk_raw = raw[:, QK0].rearrange("p (c n) -> p c n", c=C)
        fa_raw = raw[:, QK1, 0:C * ER].rearrange("p (c n) -> p c n", c=C)
        bm_sb = flat_v0[:, 0:D]
        fb_sb = raw[:, WO, 0:D]
        y_sb = [flat_q[:, i * D:(i + 1) * D] for i in range(2)]
        resid_b = [flat_q[:, (2 + i) * D:(3 + i) * D] for i in range(2)]
        qka_sb = [flat_k[:, i * QKA:(i + 1) * QKA] for i in range(2)]
        prod = flat_k[:, 2 * QKA:2 * QKA + E * DK]
        at = 2 * QKA + E * DK
        u_sb = [flat_k[:, at + i * ER:at + (i + 1) * ER] for i in range(2)]

        def flat_w(t, head):
            return t[:, head].rearrange("p a c n -> p (a c n)")

        bm_hi, bm_lo = flat_w(wqk_hi, 0)[:, 0:D], flat_w(wqk_lo, 0)[:, 0:D]
        u_hi = [flat_w(wqk_hi, 1)[:, i * P:(i + 1) * P] for i in range(2)]
        u_lo = [flat_w(wqk_lo, 1)[:, i * P:(i + 1) * P] for i in range(2)]
        router = sb("router", [P, 2, E], F32)
        router_e = sb("router_e", [P, 2, E], F32)
        router_nm = sb("router_nm", [P, 2], F32)
        router_sum = sb("router_sum", [P, 2], F32)
        router_inv = sb("router_inv", [P, 2], F32)

        def bank(name):
            return ctx.enter_context(nc.psum_tensor(name, [P, 512], F32))

        ps_q, ps_k, ps_v, ps_s, ps_pt, ps_pv, ps_o0, ps_o1 = [
            bank(n) for n in ("ps_q", "ps_k", "ps_v", "ps_s", "ps_pt", "ps_pv", "ps_o0", "ps_o1")]
        ps_o = (ps_o0, ps_o1)
        ps_x = (ps_o0, ps_o1, ps_s, ps_pt)
        ps_w = (ps_q, ps_k)
        ps_a = (ps_s, ps_pt)
        ps_yt, ps_ut = ps_v, ps_pv

        ctx_in = [sem(f"ctx_in{i}") for i in range(C + 1)]
        x_in = [sem(f"x_in{i}") for i in range(2)]
        small_in = sem("small_in")
        raw_in = [sem(f"raw_in{i}") for i in range(4)]
        k_raw_in = [sem(f"k_raw_in{i}") for i in range(HG)]
        bias_in = [sem("bias_in0"), sem("bias_in1")]
        fq_in, fw_in, fka_in = sem("fq_in"), sem("fw_in"), sem("fka_in")
        bm_in = sem("bm_in")
        bm_hi_done, bm_lo_done = sem("bm_hi_done"), sem("bm_lo_done")
        bvec_in = sem("bvec_in")
        stored = sem("stored")
        w_hi_done = [sem(f"w_hi_done{i}") for i in range(4)]
        w_lo_done = [sem(f"w_lo_done{i}") for i in range(4)]
        k0_hi_done = sem("k0_hi_done")
        k0_lo_done = sem("k0_lo_done")
        f_hi_done = sem("f_hi_done")
        f_lo_done = sem("f_lo_done")
        ident_zero = sem("ident_zero")
        consts_ready = sem("consts_ready")
        mask_ready = sem("mask_ready")
        c_hi_done = sem("c_hi_done")
        c_lo_done = sem("c_lo_done")
        stats_done = sem("stats_done")
        aggr_done = sem("aggr_done")
        var_done = sem("var_done")
        root_done = sem("root_done")
        hidden_done = sem("hidden_done")
        resid_done = sem("resid_done")
        normed_done = sem("normed_done")
        xt_done = sem("xt_done")
        x_hi_done = sem("x_hi_done")
        x_lo_done = sem("x_lo_done")
        q_done, k_done, v_done = sem("q_done"), sem("k_done"), sem("v_done")
        q_ready, k_ready, v_ready = sem("q_ready"), sem("k_ready"), sem("v_ready")
        bm_ready = sem("bm_ready")
        scores_done = sem("scores_done")
        scores_read = sem("scores_read")
        max_done = sem("max_done")
        exp_done = sem("exp_done")
        inv_done = sem("inv_done")
        probs_ready = sem("probs_ready")
        probs_turned = sem("probs_turned")
        pt_done = sem("pt_done")
        pt_copied = sem("pt_copied")
        pv_done = sem("pv_done")
        at_hi_done = sem("at_hi_done")
        at_lo_done = sem("at_lo_done")
        o_done = sem("o_done")
        o_added = sem("o_added")
        f_stats, f_aggr, f_eps, f_rstd = sem("f_stats"), sem("f_aggr"), sem("f_eps"), sem("f_rstd")
        y_done, yt_done, yt_hi, yt_lo = sem("y_done"), sem("yt_done"), sem("yt_hi"), sem("yt_lo")
        resid_b_done = sem("resid_b_done")
        fa_done, fa_copied = sem("fa_done"), sem("fa_copied")
        prod_done, route_sum, route_scaled = sem("prod_done"), sem("route_sum"), sem("route_scaled")
        route_max, route_exp, route_inv = sem("route_max"), sem("route_exp"), sem("route_inv")
        u_done, ut_done, ut_hi, ut_lo = sem("u_done"), sem("ut_done"), sem("ut_hi"), sem("ut_lo")
        fo_done, result_done = sem("fo_done"), sem("result_done")

        def per_group(engine, step):
            step(0, 0)
            with engine.Fori(1, G - 4, 2) as g:
                step(g, 1)
                step(g + 1, 0)
            for g in range(G - 3, G):
                step(g, g % 2)

        def exists(group):
            return not isinstance(group, int) or group < G

        block = ctx.enter_context(nc.Block())

        @block.sync
        def _(sp):
            def load(kind, g):
                if kind in (QK0, QK1):
                    h = HG * g + kind
                    sp.dma_start(raw[:, kind, 0:512], wq[h]).then_inc(raw_in[kind], 16)
                    sp.dma_start(raw[:, kind, 512:1024], wk[h]).then_inc(k_raw_in[kind], 16)
                elif kind == WV:
                    sp.dma_start(raw[:, WV, :], wv[g]).then_inc(raw_in[WV], 16)
                else:
                    sp.dma_start(raw[:, WO, :], wo[g]).then_inc(raw_in[WO], 16)

            def load_bias(g, p):
                sp.dma_start(bias_sb[:, p], bias[g]).then_inc(bias_in[p], 16)

            def load_x(half):
                bs = slice(HALF * half, HALF * (half + 1))
                sp.dma_start(resid[:, bs, :], x[bs].rearrange("b p d -> p b d")).then_inc(x_in[half], 16)

            for c in range(C):
                sp.dma_start(ctx_raw[0][:, c, :], ctx_t[:, 0, c]).then_inc(ctx_in[c], 16)
                if c == 0:
                    sp.dma_start(raw[:, QK0, 512:1024], wk[0]).then_inc(k_raw_in[0], 16)
            load(WV, 0)
            sp.dma_start(raw[:, QK1, 512:1024], wk[1]).then_inc(k_raw_in[1], 16)
            load_x(0)
            sp.dma_start(ctx_raw[1], ctx_t[:, 1]).then_inc(ctx_in[C], 16)
            sp.dma_start(mask_raw, mask).then_inc(small_in, 16)
            sp.dma_start(ln_sb[:, :], ln_w).then_inc(small_in, 16)
            for h in range(HG):
                sp.dma_start(raw[:, QK0 + h, 0:512], wq[h]).then_inc(raw_in[QK0 + h], 16)
            load_x(1)
            load_bias(0, 0)
            load_bias(1, 1)
            sp.wait_ge(w_lo_done[WV], 1)
            load(WV, 1)
            sp.wait_ge(w_lo_done[QK0], 1)
            load(QK0, 1)
            sp.wait_ge(w_lo_done[QK1], 1)
            load(QK1, 1)
            load(WO, 0)
            sp.wait_ge(w_lo_done[WV], 2)
            load(WV, 2)
            sp.wait_ge(w_lo_done[QK0], 2)
            load(QK0, 2)

            def step(g, p):
                if exists(g + 2):
                    sp.wait_ge(w_lo_done[QK1], g + 2)
                    load(QK1, g + 2)
                if exists(g + 3):
                    sp.wait_ge(w_lo_done[WV], g + 3)
                    load(WV, g + 3)
                if isinstance(g, int) and g == G - 2:
                    sp.wait_ge(w_lo_done[WV], G)
                    sp.dma_start(fq_raw, f_wq).then_inc(fq_in, 16)
                    sp.wait_ge(w_lo_done[QK0], G)
                    sp.wait_ge(w_lo_done[QK1], G)
                    sp.dma_start(fw_raw, f_w).then_inc(fw_in, 16)
                if exists(g + 1):
                    sp.wait_ge(w_lo_done[WO], g + 1)
                    load(WO, g + 1)
                if isinstance(g, int) and g == G - 2:
                    sp.wait_ge(f_lo_done, 2)
                    sp.dma_start(fk_raw, f_wk).then_inc(fka_in, 16)
                    sp.dma_start(fa_raw, f_a).then_inc(fka_in, 16)
                if exists(g + 2):
                    sp.wait_ge(bm_ready, NB * g + NB)
                    load_bias(g + 2, p)
                if exists(g + 3):
                    sp.wait_ge(w_lo_done[QK0], g + 3)
                    load(QK0, g + 3)
                if isinstance(g, int) and g == G - 1:
                    sp.wait_ge(pv_done, BLOCKS - NB)
                    sp.dma_start(bm_sb, f_bm).then_inc(bm_in, 16)
                    sp.wait_ge(w_lo_done[WO], G)
                    sp.dma_start(fb_sb, f_b.to_broadcast([P, D])).then_inc(bvec_in, 16)

            per_group(sp, step)
            for b in range(B):
                sp.wait_ge(result_done, b + 1)
                sp.dma_start(out[b], resid[:, b, :]).then_inc(stored, 16)
            sp.wait_ge(stored, 16 * B)

        @block.gpsimd
        def _(pool):
            nc.gpsimd.memset(ident[:, :], 0.0).then_inc(ident_zero, 1)
            pool.wait_ge(ident_zero, 1)
            nc.gpsimd.affine_select(out=ident[:, :], in_=ident[:, :], compare_op=ALU.not_equal, fill=1.0,
                                    base=0, pattern=[[-1, P]], channel_multiplier=1).then_inc(consts_ready, 1)
            nc.gpsimd.memset(minus_half[:, :, :], -0.5).then_inc(consts_ready, 1)
            pool.wait_ge(consts_ready, 2)
            for half in range(2):
                bs = slice(HALF * half, HALF * (half + 1))
                pool.wait_ge(var_done, 2 * (half + 1))
                nc.gpsimd.tensor_tensor(inv_root[:, :, bs], variances[:, :, bs], minus_half[:, :, bs],
                                        ALU.pow).then_inc(root_done, 1)
            pool.wait_ge(mask_ready, 1)

            def add_hidden(b):
                pool.wait_ge(hidden_done, b + 1)
                nc.gpsimd.tensor_tensor(resid[:, b, :], resid[:, b, :], x_normed[:, b % HALF, :],
                                        ALU.add).then_inc(resid_done, 1)

            def bias_and_mask(s, g, j, p):
                if not isinstance(s, int) or s >= 2:
                    pool.wait_ge(scores_read, s - 1)
                head, half = j % 2, j // 2
                one = bias_sb[:, p, head:head + 1, :].to_broadcast([P, HALF, P])
                nc.gpsimd.tensor_tensor(bias_mask[:, j % 2], one,
                                        mask_neg[:, HALF * half:HALF * (half + 1), :], ALU.add).then_inc(bm_ready, 1)

            def step(g, p):
                if isinstance(g, int):
                    pool.wait_ge(bias_in[p], 16 * (g // 2 + 1))
                else:
                    pool.wait_ge(bias_in[p], 8 * (g - p) + 16)
                for j in range(NB):
                    bias_and_mask(NB * g + j, g, j, p)
                    if isinstance(g, int) and g == 0 and j == 1:
                        for b in range(B):
                            add_hidden(b)

            per_group(pool, step)
            pool.wait_ge(bvec_in, 16)

            def inverse_deviation(b):
                pool.wait_ge(f_eps, b + 1)
                nc.gpsimd.tensor_tensor(rstd[:, b:b + 1], variances[:, 0, b:b + 1], minus_half[:, 0, 0:1], ALU.pow).then_inc(f_rstd, 1)

            inverse_deviation(0)
            inverse_deviation(1)
            for b in range(B):
                if b >= 2:
                    pool.wait_ge(result_done, b - 1)
                nc.gpsimd.tensor_tensor(resid_b[b % 2], resid[:, b, :], fb_sb, ALU.add).then_inc(resid_b_done, 1)
                if b + 2 < B:
                    inverse_deviation(b + 2)

        def weight_parts(kind, p):
            def flat(t):
                names = " ".join("abcd"[:len(t.shape) - 1])
                return t.rearrange(f"p {names} -> p ({names})")
            if kind in (QK0, QK1):
                return raw[:, kind], flat(wqk_hi[:, kind]), flat(wqk_lo[:, kind])
            if kind == WV:
                return raw[:, WV], flat(wv_hi[:, p]), flat(wv_lo[:, p])
            return raw[:, WO], flat(wo_hi[:, p]), flat(wo_lo[:, p])

        def output_banks(n, last):
            return (ps_q, ps_k) if last and n % 2 else ps_o

        def v_of_slot(j, g):
            if isinstance(g, int) and g == G - 1:
                return {0: (BLOCKS - 2, 2), 2: (BLOCKS - 1, 3)}.get(j)
            if isinstance(g, int) and g == G - 2 and j >= 2:
                return None
            return NB * (g + 1) + j, j

        def slot_weights(j, g, p):
            kinds = [(QK1, g + 1, 0), (WV, g + 2, p), (WO, g, p), (QK0, g + 2, 0)]
            if isinstance(g, int) and g == G - 1:
                kinds[0], kinds[2] = kinds[2], kinds[0]
            return kinds[j]

        @block.scalar
        def _(act):
            def copy(o, i):
                return nc.scalar.activation(o, i, ACT.Copy)

            def split_hi(kind, group, p):
                act.wait_ge(raw_in[kind], 16 * (group + 1))
                if kind in (QK0, QK1):
                    act.wait_ge(k_raw_in[kind], 16 * (group + 1))
                r, hi, _ = weight_parts(kind, p)
                copy(hi, r).then_inc(w_hi_done[kind], 1)

            def q_out(n, j, bank=ps_q):
                act.wait_ge(q_done, n + 1)
                copy(q_t[:, j % 2, TOK * (j // 2):TOK * (j // 2 + 1)], bank[:, :]).then_inc(q_ready, 1)

            def k_out(n, j):
                act.wait_ge(k_done, n + 1)
                copy(k_t[:, j % 2, TOK * (j // 2):TOK * (j // 2 + 1)], ps_k[:, :]).then_inc(k_ready, 1)

            def v_out(n, j, p):
                act.wait_ge(v_done, n + 1)
                copy(v_sb[:, p, 2 * j:2 * j + 2, :].rearrange("p b n -> p (b n)"), ps_v[:, :]).then_inc(v_ready, 1)

            def x_high(n):
                half, c = n // C, n % C
                act.wait_ge(xt_done, n + 1)
                nc.scalar.activation(x_hi[:, c, TOK * half:TOK * (half + 1)], ps_x[c][:, :], ACT.Copy,
                                     scale=ln_sb[:, c:c + 1]).then_inc(x_hi_done, 1)

            def k0_hi(h):
                act.wait_ge(k_raw_in[h], 16)
                copy(wqk_hi[:, h, 1].rearrange("p c n -> p (c n)"), raw[:, QK0 + h, 512:1024]).then_inc(k0_hi_done, 1)

            def q0_hi(h):
                act.wait_ge(raw_in[QK0 + h], 16)
                copy(wqk_hi[:, h, 0].rearrange("p c n -> p (c n)"), raw[:, QK0 + h, 0:512]).then_inc(w_hi_done[h], 1)

            for c in range(C):
                act.wait_ge(ctx_in[c], 16)
                copy(c_hi[:, c, 0:TOK], ctx_raw[0][:, c, :]).then_inc(c_hi_done, 1)
                if c == 0:
                    k0_hi(0)
            split_hi(WV, 0, 0)
            k0_hi(1)
            k_out(0, 0)
            v_out(0, 0, 0)
            act.wait_ge(ctx_in[C], 16)
            copy(c_hi[:, :, TOK:2 * TOK], ctx_raw[1]).then_inc(c_hi_done, 1)
            k_out(1, 1)
            v_out(1, 1, 0)
            for h in range(HG):
                q0_hi(h)
            k_out(2, 2)
            act.wait_ge(small_in, 32)
            for n in range(C):
                x_high(n)
            v_out(2, 2, 0)
            k_out(3, 3)
            q_out(0, 0)
            split_hi(WV, 1, 1)
            v_out(3, 3, 0)
            for n in range(C, 2 * C):
                x_high(n)
            q_out(1, 1)
            q_out(2, 2, ps_o0)
            split_hi(QK0, 1, 0)
            q_out(3, 3)

            def ffn_split_hi(j):
                if j == 1:
                    act.wait_ge(fq_in, 16)
                    act.wait_ge(v_done, BLOCKS - NB)
                    copy(fq_hi, fq_raw).then_inc(f_hi_done, 1)
                elif j == 2:
                    act.wait_ge(fw_in, 16)
                    act.wait_ge(q_done, BLOCKS - 2)
                    copy(fw_hi, fw_raw).then_inc(f_hi_done, 1)
                else:
                    act.wait_ge(fka_in, 32)
                    act.wait_ge(k_done, BLOCKS - 2)
                    act.wait_ge(v_done, BLOCKS - 2)
                    copy(fka_hi[:, :, 0:E * DK], fk_raw)
                    copy(fka_hi[:, :, E * DK:KA], fa_raw).then_inc(f_hi_done, 1)

            def step(g, p):
                s0 = NB * g
                last = isinstance(g, int) and g == G - 1
                for j in range(NB):
                    s = s0 + j
                    kind, group, wp = slot_weights(j, g, p)
                    if exists(group):
                        if kind in (QK0, QK1):
                            act.wait_ge(k_done, s + 4)
                        elif kind == WV:
                            act.wait_ge(v_done, s + 3)
                        elif not isinstance(g, int) or g >= 2:
                            act.wait_ge(o_done, s0 - 4)
                        split_hi(kind, group, wp)
                    if isinstance(g, int) and g == G - 2 and j > 0:
                        ffn_split_hi(j)
                    if last and j > 0:
                        probs_out(j)
                    act.wait_ge(max_done, s + 1)
                    for i in range(HALF):
                        e = nc.scalar.activation(probs[:, j % 2, i, :], probs[:, j % 2, i, :], ACT.Exp,
                                                 bias=neg_max[:, j % 2, i:i + 1],
                                                 accum_out=row_sum[:, j % 2, i:i + 1])
                    e.then_inc(exp_done, 1)
                    if not last:
                        q_out(s + NB, j)
                    if not isinstance(s, int) or s > 0:
                        at_high(s, j)
                    if not last:
                        k_out(s + NB, j)
                    if v_of_slot(j, g):
                        if isinstance(g, int) and g == 0 and j == 0:
                            act.wait_ge(resid_done, B)
                        v_out(*v_of_slot(j, g), p if last else 1 - p)

            def probs_out(n):
                act.wait_ge(pt_done, n)
                copy(probs_t[:, :], ps_pt[:, :]).then_inc(pt_copied, 1)

            def at_high(s, j):
                jj = (j - 1) % NB
                act.wait_ge(pv_done, s)
                copy(at_hi[:, jj % 2, TOK * (jj // 2):TOK * (jj // 2 + 1)], ps_pv[:, :]).then_inc(at_hi_done, 1)

            per_group(act, step)
            probs_out(NB)
            at_high(BLOCKS, 0)

            def yt_high(b):
                act.wait_ge(yt_done, b + 1)
                copy(x_hi[:, :, D + P * (b % 2):D + P * (b % 2 + 1)],
                     ps_yt[:, :].rearrange("p (c t) -> p c t", c=C)).then_inc(yt_hi, 1)

            yt_high(0)
            act.wait_ge(bm_in, 16)
            copy(bm_hi, bm_sb).then_inc(bm_hi_done, 1)
            yt_high(1)
            for b in range(B):
                act.wait_ge(fa_done, b + 1)
                if b >= 2:
                    act.wait_ge(u_done, b - 1)
                for i, (lo, hi) in enumerate(((0, E * DK), (E * DK, QKA))):
                    a = copy(qka_sb[b % 2][:, lo:hi], ps_a[i][:, 0:hi - lo])
                a.then_inc(fa_copied, 1)
                act.wait_ge(route_max, b + 1)
                nc.scalar.activation(router_e[:, b % 2, :], router[:, b % 2, :], ACT.Exp,
                                     bias=router_nm[:, b % 2:b % 2 + 1],
                                     accum_out=router_sum[:, b % 2:b % 2 + 1]).then_inc(route_exp, 1)
                if b + 2 < B:
                    yt_high(b + 2)
                act.wait_ge(ut_done, b + 1)
                copy(u_hi[b % 2], ps_ut[:, 0:P]).then_inc(ut_hi, 1)

        @block.vector
        def _(dve):
            def sub(o, a, hi):
                return nc.vector.tensor_tensor(o, a, hi.bitcast(F32), ALU.subtract)

            def split_lo(kind, group, p):
                dve.wait_ge(w_hi_done[kind], group + 1)
                r, hi, lo = weight_parts(kind, p)
                sub(lo, r, hi).then_inc(w_lo_done[kind], 1)

            def tile_stats(b, n, done, aggregated):
                if n > 0:
                    dve.wait_ge(aggregated, n)
                nc.vector.bn_stats(stats[:, :], resid[:, b, :]).then_inc(done, 1)
                dve.wait_ge(done, n + 1)
                nc.vector.bn_aggr(mean_var[:, b, :], stats[:, :]).then_inc(aggregated, 1)

            def x_low(n):
                half, c = n // C, n % C
                ts = slice(TOK * half, TOK * (half + 1))
                dve.wait_ge(x_hi_done, n + 1)
                nc.vector.scalar_tensor_tensor(out=x_lo[:, c, ts], in0=ps_x[c][:, :], scalar=ln_sb[:, c:c + 1],
                                               in1=x_hi[:, c, ts].bitcast(F32), op0=ALU.mult,
                                               op1=ALU.subtract).then_inc(x_lo_done, 1)

            def c_low(n, c, ts, src):
                dve.wait_ge(c_hi_done, n)
                sub(c_lo[:, c, ts], src, c_hi[:, c, ts]).then_inc(c_lo_done, 1)

            def k0_lo(h):
                dve.wait_ge(k0_hi_done, h + 1)
                sub(wqk_lo[:, h, 1].rearrange("p c n -> p (c n)"), raw[:, QK0 + h, 512:1024],
                    wqk_hi[:, h, 1].rearrange("p c n -> p (c n)")).then_inc(k0_lo_done, 1)

            def q0_lo(h):
                dve.wait_ge(w_hi_done[h], 1)
                sub(wqk_lo[:, h, 0].rearrange("p c n -> p (c n)"), raw[:, QK0 + h, 0:512],
                    wqk_hi[:, h, 0].rearrange("p c n -> p (c n)")).then_inc(w_lo_done[h], 1)

            def half_stats(half):
                bs = slice(HALF * half, HALF * (half + 1))
                dve.wait_ge(x_in[half], 16)
                for b in range(HALF * half, HALF * (half + 1)):
                    tile_stats(b, b, stats_done, aggr_done)
                dve.wait_ge(aggr_done, HALF * (half + 1))
                nc.vector.tensor_scalar(variances[:, 0, bs], mean_var[:, bs, 1], EPS, None, ALU.add).then_inc(var_done, 1)
                nc.vector.tensor_scalar(variances[:, 1, bs], mean_var[:, bs, 1], 1.0 + EPS, EPS * EPS,
                                        ALU.mult, ALU.add).then_inc(var_done, 1)

            def half_normed(half):
                dve.wait_ge(root_done, half + 1)
                if half == 0:
                    dve.wait_ge(c_lo_done, C)
                else:
                    dve.wait_ge(xt_done, C)
                for b in range(HALF * half, HALF * (half + 1)):
                    nc.vector.tensor_scalar(x_normed[:, b % HALF, :], resid[:, b, :], mean_var[:, b, 0:1],
                                            norm_rms[:, b:b + 1], ALU.subtract, ALU.mult).then_inc(normed_done, 1)

            def hidden(b):
                if b >= HALF:
                    dve.wait_ge(resid_done, b - HALF + 1)
                nc.vector.tensor_scalar(x_normed[:, b % HALF, :], resid[:, b, :], mean_var[:, b, 0:1],
                                        rstd[:, b:b + 1], ALU.subtract, ALU.mult).then_inc(hidden_done, 1)

            for c in range(C):
                c_low(c + 1, c, slice(0, TOK), ctx_raw[0][:, c, :])
                if c == 0:
                    k0_lo(0)
            split_lo(WV, 0, 0)
            k0_lo(1)
            half_stats(0)
            dve.wait_ge(small_in, 32)
            nc.vector.tensor_scalar(mask_neg[:, :, :].rearrange("p b k -> p (b k)"), mask_raw, -1.0, MASKED,
                                    ALU.add, ALU.mult).then_inc(mask_ready, 1)
            c_low(C + 1, slice(0, C), slice(TOK, 2 * TOK), ctx_raw[1])
            half_normed(0)
            for h in range(HG):
                q0_lo(h)
            for n in range(C):
                x_low(n)
            half_stats(1)
            nc.vector.tensor_reduce(row_valid[:, :], mask_raw.rearrange("p (b k) -> p b k", b=B),
                                    AX_X, ALU.max).then_inc(mask_ready, 1)
            half_normed(1)
            split_lo(WV, 1, 1)
            for n in range(C, 2 * C):
                x_low(n)
            dve.wait_ge(xt_done, 2 * C)
            for b in range(HALF):
                hidden(b)
            split_lo(QK0, 1, 0)
            for b in range(HALF, B):
                hidden(b)
            dve.wait_ge(mask_ready, 2)

            def add_output(n, j, last=False):
                dve.wait_ge(o_done, n + 1)
                for i in range(2):
                    a = nc.vector.tensor_tensor(resid[:, 2 * j + i, :], output_banks(n, last)[i][:, :], resid[:, 2 * j + i, :], ALU.add)
                a.then_inc(o_added, 1)

            def at_low(s, j):
                jj = (j - 1) % NB
                ts = slice(TOK * (jj // 2), TOK * (jj // 2 + 1))
                dve.wait_ge(at_hi_done, s)
                sub(at_lo[:, jj % 2, ts], ps_pv[:, :], at_hi[:, jj % 2, ts]).then_inc(at_lo_done, 1)

            def turn_probs(s, pr):
                dve.wait_ge(probs_ready, s + 1)
                if not isinstance(s, int) or s > 0:
                    dve.wait_ge(pv_done, s)
                to = probs_t[:, :].rearrange("p (b q) -> p b q", b=HALF)
                for q in range(0, P, SQUARE):
                    for k in range(0, P, SQUARE):
                        t = nc.vector.transpose(to[k:k + SQUARE, :, q:q + SQUARE], pr[q:q + SQUARE, :, k:k + SQUARE])
                t.then_inc(probs_turned, 1)

            def step(g, p):
                later = not isinstance(g, int) or g > 0
                last = isinstance(g, int) and g == G - 1
                for j in range(NB):
                    s = NB * g + j
                    half = j // 2
                    pr = probs[:, j % 2]
                    dve.wait_ge(scores_done, s + 1)
                    dve.wait_ge(bm_ready, s + 1)
                    nc.vector.tensor_tensor(pr, ps_s[:, :].rearrange("p (b k) -> p b k", b=HALF),
                                            bias_mask[:, j % 2], ALU.add).then_inc(scores_read, 1)
                    dve.wait_ge(scores_read, s + 1)
                    nc.vector.tensor_reduce(neg_max[:, j % 2, :], pr, AX_X, ALU.max, negate=True).then_inc(max_done, 1)
                    if later:
                        add_output(s - 4, j, isinstance(g, int) and g == G - 1 and j > 0)
                    kind, group, wp = slot_weights(j, g, p)
                    if exists(group):
                        split_lo(kind, group, wp)
                    if isinstance(g, int) and g == G - 2 and j > 0:
                        dve.wait_ge(f_hi_done, j)
                        if j == 1:
                            sub(fq_lo, fq_raw, fq_hi).then_inc(f_lo_done, 1)
                        elif j == 2:
                            sub(fw_lo, fw_raw, fw_hi).then_inc(f_lo_done, 1)
                        else:
                            sub(fka_lo[:, :, 0:E * DK], fk_raw, fka_hi[:, :, 0:E * DK])
                            sub(fka_lo[:, :, E * DK:KA], fa_raw, fka_hi[:, :, E * DK:KA]).then_inc(f_lo_done, 1)
                    dve.wait_ge(exp_done, s + 1)
                    nc.vector.reciprocal(row_inv[:, j % 2, :], row_sum[:, j % 2, :]).then_inc(inv_done, 1)
                    dve.wait_ge(inv_done, s + 1)
                    for i in range(HALF):
                        b = HALF * half + i
                        n = nc.vector.tensor_scalar(pr[:, i, :], pr[:, i, :], row_inv[:, j % 2, i:i + 1],
                                                    row_valid[:, b:b + 1], ALU.mult, ALU.mult)
                    n.then_inc(probs_ready, 1)
                    if later or j > 0:
                        at_low(s, j)
                    if not last:
                        turn_probs(s, pr)
                    if isinstance(g, int) and g == 0 and j == NB - 1:
                        dve.wait_ge(resid_done, B)

            per_group(dve, step)

            def normalise(b):
                tile_stats(b, b, f_stats, f_aggr)
                dve.wait_ge(f_aggr, b + 1)
                nc.vector.tensor_scalar(variances[:, 0, b:b + 1], mean_var[:, b, 1:2], EPS, None, ALU.add).then_inc(f_eps, 1)

            def normalised(b):
                dve.wait_ge(f_rstd, b + 1)
                if b >= 2:
                    dve.wait_ge(yt_done, b - 1)
                nc.vector.tensor_scalar(y_sb[b % 2], resid[:, b, :], mean_var[:, b, 0:1], rstd[:, b:b + 1],
                                        ALU.subtract, ALU.mult).then_inc(y_done, 1)

            def yt_low(b):
                ts = slice(D + P * (b % 2), D + P * (b % 2 + 1))
                dve.wait_ge(yt_hi, b + 1)
                sub(x_lo[:, :, ts], ps_yt[:, :].rearrange("p (c t) -> p c t", c=C), x_hi[:, :, ts]).then_inc(yt_lo, 1)

            def result(b):
                dve.wait_ge(fo_done, b + 1)
                dve.wait_ge(resid_b_done, b + 1)
                nc.vector.tensor_tensor(resid[:, b, :], ps_w[b % 2][:, :], resid_b[b % 2],
                                        ALU.add).then_inc(result_done, 1)

            add_output(BLOCKS - 4, 0, True)
            dve.wait_ge(o_added, BLOCKS - 3)
            normalise(0)
            at_low(BLOCKS, 0)
            normalised(0)
            add_output(BLOCKS - 3, 1, True)
            dve.wait_ge(o_added, BLOCKS - 2)
            normalise(1)
            yt_low(0)
            normalised(1)
            add_output(BLOCKS - 2, 2, True)
            add_output(BLOCKS - 1, 3, True)
            dve.wait_ge(o_added, BLOCKS)

            def u_low(b):
                dve.wait_ge(ut_hi, b + 1)
                sub(u_lo[b % 2], ps_ut[:, 0:P], u_hi[b % 2]).then_inc(ut_lo, 1)

            for b in range(B):
                if b + 1 < B:
                    yt_low(b + 1)
                if b + 2 < B:
                    normalise(b + 2)
                    normalised(b + 2)
                q = b % 2
                if b == 0:
                    dve.wait_ge(bm_hi_done, 1)
                    sub(bm_lo, bm_sb, bm_hi).then_inc(bm_lo_done, 1)
                else:
                    u_low(b - 1)
                dve.wait_ge(fa_copied, b + 1)
                nc.vector.tensor_tensor(prod, qka_sb[q][:, 0:E * DK], qka_sb[q][:, E * DK:2 * E * DK],
                                        ALU.mult).then_inc(prod_done, 1)
                dve.wait_ge(prod_done, b + 1)
                nc.vector.tensor_reduce(router[:, q, :], prod.rearrange("p (e d) -> p e d", e=E),
                                        AX_X, ALU.add).then_inc(route_sum, 1)
                dve.wait_ge(route_sum, b + 1)
                nc.vector.tensor_scalar(router[:, q, :], router[:, q, :], float(DK) ** -0.5, None,
                                        ALU.mult).then_inc(route_scaled, 1)
                dve.wait_ge(route_scaled, b + 1)
                nc.vector.tensor_reduce(router_nm[:, q:q + 1], router[:, q, :], AX_X, ALU.max,
                                        negate=True).then_inc(route_max, 1)
                dve.wait_ge(route_exp, b + 1)
                nc.vector.reciprocal(router_inv[:, q:q + 1], router_sum[:, q:q + 1]).then_inc(route_inv, 1)
                dve.wait_ge(route_inv, b + 1)
                nc.vector.scalar_tensor_tensor(
                    out=u_sb[q].rearrange("p (e r) -> p e r", e=E),
                    in0=qka_sb[q][:, 2 * E * DK:QKA].rearrange("p (e r) -> p e r", e=E),
                    scalar=router_inv[:, q:q + 1],
                    in1=router_e[:, q, :].rearrange("p (e o) -> p e o", o=1).to_broadcast([P, E, R]),
                    op0=ALU.mult, op1=ALU.mult).then_inc(u_done, 1)
                if b > 0:
                    result(b - 1)
            u_low(B - 1)
            result(B - 1)

        @block.tensor
        def _(pe):
            def passes(o, terms):
                for n, (lh, ll, rh, rl) in enumerate(terms):
                    pe.matmul(o, lh, rh, start=(n == 0), stop=False)
                    pe.matmul(o, lh, rl, start=False, stop=False)
                    m = pe.matmul(o, ll, rh, start=False, stop=(n == len(terms) - 1))
                return m

            def project(o, which, head, a_hi, a_lo, half):
                ts = slice(TOK * half, TOK * (half + 1))
                return passes(o, [(wqk_hi[:, head, which, c, :], wqk_lo[:, head, which, c, :],
                                   a_hi[:, c, ts], a_lo[:, c, ts]) for c in range(C)])

            def q_block(n, j, weights, into=ps_q):
                if j < 2:
                    pe.wait_ge(w_lo_done[QK0 + j % 2], weights)
                if isinstance(n, int) and n == 3:
                    pe.wait_ge(q_ready, 2)
                elif not isinstance(n, int) or n not in (0, 2):
                    pe.wait_ge(q_ready, n)
                project(into[:, :], 0, j % 2, x_hi, x_lo, j // 2).then_inc(q_done, 1)

            def k_block(n, j):
                if not isinstance(n, int) or n > 0:
                    pe.wait_ge(k_ready, n)
                project(ps_k[:, :], 1, j % 2, c_hi, c_lo, j // 2).then_inc(k_done, 1)

            def first_k_block():
                ts = slice(0, TOK)
                pe.wait_ge(k0_hi_done, 1)
                for c in range(C):
                    hi, lo = wqk_hi[:, 0, 1, c, :], wqk_lo[:, 0, 1, c, :]
                    pe.wait_ge(c_hi_done, c + 1)
                    pe.matmul(ps_k[:, :], hi, c_hi[:, c, ts], start=(c == 0), stop=False)
                    pe.wait_ge(c_lo_done, c + 1)
                    pe.matmul(ps_k[:, :], hi, c_lo[:, c, ts], start=False, stop=False)
                    if c == 0:
                        pe.wait_ge(k0_lo_done, 1)
                    m = pe.matmul(ps_k[:, :], lo, c_hi[:, c, ts], start=False, stop=(c == C - 1))
                m.then_inc(k_done, 1)

            def v_block(n, j, p, weights):
                if j == 0:
                    pe.wait_ge(w_lo_done[WV], weights)
                if not isinstance(n, int) or n > 0:
                    pe.wait_ge(v_ready, n)
                for i in range(2):
                    ts = slice(P * (2 * j + i), P * (2 * j + i + 1))
                    m = passes(ps_v[:, HG * P * i:HG * P * (i + 1)],
                               [(c_hi[:, c, ts], c_lo[:, c, ts], wv_hi[:, p, c, :], wv_lo[:, p, c, :])
                                for c in range(C)])
                m.then_inc(v_done, 1)

            def x_transposes(half):
                pe.wait_ge(normed_done, HALF * (half + 1))
                for c in range(C):
                    if half > 0:
                        pe.wait_ge(x_lo_done, c + 1)
                    for i in range(HALF):
                        m = pe.transpose(ps_x[c][:, P * i:P * (i + 1)], x_normed[:, i, P * c:P * (c + 1)],
                                         ident[:, :])
                    m.then_inc(xt_done, 1)

            def scores(s, j):
                head, half = j % 2, j // 2
                pe.wait_ge(q_ready, s + 1)
                pe.wait_ge(k_ready, s + 1)
                if not isinstance(s, int) or s > 0:
                    pe.wait_ge(scores_read, s)
                for i in range(HALF):
                    ts = slice(TOK * half + P * i, TOK * half + P * (i + 1))
                    m = pe.matmul(ps_s[:, P * i:P * (i + 1)], q_t[:, head, ts], k_t[:, head, ts],
                                  start=True, stop=True)
                m.then_inc(scores_done, 1)

            pe.wait_ge(consts_ready, 2)
            first_k_block()
            v_block(0, 0, 0, 1)
            pe.wait_ge(k0_lo_done, 2)
            k_block(1, 1)
            v_block(1, 1, 0, 1)
            pe.wait_ge(c_lo_done, C + 1)
            k_block(2, 2)
            x_transposes(0)
            v_block(2, 2, 0, 1)
            k_block(3, 3)
            pe.wait_ge(x_lo_done, C)
            q_block(0, 0, 1)
            v_block(3, 3, 0, 1)
            x_transposes(1)
            q_block(1, 1, 1)
            pe.wait_ge(x_lo_done, 2 * C)
            q_block(2, 2, 1, ps_o0)
            q_block(3, 3, 1)
            scores(0, 0)

            def turn_probs(s, j):
                pe.wait_ge(probs_ready, s)
                if s > BLOCKS - NB + 1:
                    pe.wait_ge(pt_copied, s - 1 - (BLOCKS - NB))
                for i in range(HALF):
                    m = pe.transpose(ps_pt[:, P * i:P * (i + 1)], probs[:, (j - 1) % 2, i, :], ident[:, :])
                m.then_inc(pt_done, 1)

            def probs_v(s, j, p):
                jj = (j - 1) % NB
                vp = p if j > 0 else 1 - p
                if isinstance(s, int) and s > BLOCKS - NB:
                    pe.wait_ge(pt_copied, s - (BLOCKS - NB))
                else:
                    pe.wait_ge(probs_turned, s)
                pe.wait_ge(v_ready, s - jj + 1 + 2 * (jj // 2))
                if not isinstance(s, int) or s > 1:
                    pe.wait_ge(at_lo_done, s - 1)
                for i in range(HALF):
                    m = pe.matmul(ps_pv[:, P * i:P * (i + 1)],
                                  v_sb[:, vp, HALF * (jj // 2) + i, P * (jj % 2):P * (jj % 2 + 1)],
                                  probs_t[:, P * i:P * (i + 1)], start=True, stop=True)
                m.then_inc(pv_done, 1)

            def output_pair(n, j, p, weights=0, last=False, tiles=(0, 1)):
                nj = (j + 1) % NB
                wp = p if j == 3 else 1 - p
                if nj == 0:
                    pe.wait_ge(w_lo_done[WO], weights)
                pe.wait_ge(at_lo_done, n - nj + 2 + 2 * (nj // 2))
                if last and n == BLOCKS - 7:
                    pe.wait_ge(q_ready, BLOCKS)
                    pe.wait_ge(k_ready, BLOCKS)
                elif last:
                    pe.wait_ge(o_added, n - 1)
                elif not isinstance(n, int) or n > 0:
                    pe.wait_ge(o_added, n)
                banks = output_banks(n, last)
                for i in tiles:
                    ts = slice(P * (2 * nj + i), P * (2 * nj + i + 1))
                    m = passes(banks[i][:, :], [(at_hi[:, h, ts], at_lo[:, h, ts], wo_hi[:, wp, h, :],
                                                wo_lo[:, wp, h, :]) for h in range(HG)])
                if 1 in tiles:
                    m.then_inc(o_done, 1)

            def step(g, p):
                first = isinstance(g, int) and g == 0
                last = isinstance(g, int) and g == G - 1
                for j in range(NB):
                    s = NB * g + j
                    if not first or j > 0:
                        scores(s, j)
                    if not last:
                        q_block(s + NB, j, g + 2)
                    if last and j > 0:
                        turn_probs(s, j)
                    if last:
                        output_pair(s - 3, j, p, g + 1, True)
                    if not first or j > 0:
                        probs_v(s, j, p)
                    if not last:
                        k_block(s + NB, j)
                    if v_of_slot(j, g):
                        v_block(*v_of_slot(j, g), p if last else 1 - p, g + 2)
                    if not last and (not first or j == 3):
                        output_pair(s - 3, j, p, g + 1)

            per_group(pe, step)
            turn_probs(BLOCKS, 0)
            output_pair(BLOCKS - 3, 0, 0, last=True, tiles=(0,))
            probs_v(BLOCKS, 0, 0)
            output_pair(BLOCKS - 3, 0, 0, last=True, tiles=(1,))

            def y_transposes(b):
                pe.wait_ge(y_done, b + 1)
                if b > 0:
                    pe.wait_ge(yt_lo, b)
                for c in range(C):
                    m = pe.transpose(ps_yt[:, P * c:P * (c + 1)], y_sb[b % 2][:, P * c:P * (c + 1)], ident[:, :])
                m.then_inc(yt_done, 1)

            def yt(b):
                ts = slice(D + P * (b % 2), D + P * (b % 2 + 1))
                return [(x_hi[:, c, ts], x_lo[:, c, ts]) for c in range(C)]

            def add_adapters(b):
                o = ps_w[b % 2][:, :]
                if b == 0:
                    pe.wait_ge(bm_lo_done, 1)
                pe.wait_ge(ut_hi, b + 1)
                pe.matmul(o, u_hi[b % 2], bm_hi, start=False, stop=False)
                pe.matmul(o, u_hi[b % 2], bm_lo, start=False, stop=False)
                pe.wait_ge(ut_lo, b + 1)
                pe.matmul(o, u_lo[b % 2], bm_hi, start=False, stop=True).then_inc(fo_done, 1)

            output_pair(BLOCKS - 2, 1, 0, last=True)
            y_transposes(0)
            output_pair(BLOCKS - 1, 2, 0, last=True)
            y_transposes(1)
            pe.wait_ge(f_lo_done, 3)
            for b in range(B):
                pe.wait_ge(yt_lo, b + 1)
                if b > 0:
                    pe.wait_ge(fa_copied, b)
                for i, (hi, lo, n) in enumerate(((fq_hi, fq_lo, E * DK), (fka_hi, fka_lo, KA))):
                    m = passes(ps_a[i][:, 0:n], [(*yt(b)[c], hi[:, c, :], lo[:, c, :]) for c in range(C)])
                m.then_inc(fa_done, 1)
                if b > 0:
                    pe.wait_ge(u_done, b)
                    pe.transpose(ps_ut[:, 0:P], u_sb[(b - 1) % 2], ident[:, :]).then_inc(ut_done, 1)
                if b >= 2:
                    pe.wait_ge(result_done, b - 1)
                elif b == 0:
                    pe.wait_ge(o_added, BLOCKS)
                for c in range(C):
                    yh, yl = yt(b)[c]
                    pe.matmul(ps_w[b % 2][:, :], yh, fw_hi[:, c, :], start=(c == 0), stop=False)
                    pe.matmul(ps_w[b % 2][:, :], yh, fw_lo[:, c, :], start=False, stop=False)
                    pe.matmul(ps_w[b % 2][:, :], yl, fw_hi[:, c, :], start=False, stop=False)
                if b > 0:
                    add_adapters(b - 1)
                if b + 2 < B:
                    y_transposes(b + 2)
            b = B - 1
            pe.wait_ge(u_done, b + 1)
            pe.transpose(ps_ut[:, 0:P], u_sb[b % 2], ident[:, :]).then_inc(ut_done, 1)
            add_adapters(b)


def kernel(x, ctx_4096, mask_BxSxS2_bk0, L0_xattn_position_bias, L0_xattn_ln_weight, L0_xattn_w_q,
           L0_xattn_w_k, L0_xattn_w_v, L0_xattn_w_out, L0_ffn_W, L0_ffn_b, L0_ffn_Wq, L0_ffn_Wk,
           L0_ffn_A, L0_ffn_Bm):
    import numpy as np
    import concourse.bacc as bacc
    from concourse.bass_utils import run_bass_kernel_spmd

    def heads(w):
        return np.asarray(w).reshape(H, P, C, P).transpose(0, 3, 2, 1).reshape(H, P, C * P)

    def turned(w):
        w = np.asarray(w)
        return w.reshape(w.shape[0], C, P).transpose(2, 1, 0)

    laid = {
        "x": np.asarray(x),
        "ctx_t": np.asarray(ctx_4096).reshape(2, TOK, C, P).transpose(3, 0, 2, 1),
        "mask": np.asarray(mask_BxSxS2_bk0).transpose(1, 0, 2).reshape(P, B * P),
        "bias": np.asarray(L0_xattn_position_bias).reshape(G, HG, P, P).transpose(0, 2, 1, 3),
        "ln_w": np.asarray(L0_xattn_ln_weight).reshape(C, P).T,
        "wq": heads(L0_xattn_w_q),
        "wk": heads(L0_xattn_w_k),
        "wv": np.asarray(L0_xattn_w_v).reshape(G, HG * P, C, P).transpose(0, 3, 2, 1).reshape(G, P, C * HG * P),
        "wo": np.asarray(L0_xattn_w_out).reshape(D, G, HG, P).transpose(1, 3, 2, 0).reshape(G, P, HG * D),
        "f_w": turned(L0_ffn_W),
        "f_b": np.asarray(L0_ffn_b).reshape(1, D),
        "f_wq": turned(L0_ffn_Wq),
        "f_wk": turned(L0_ffn_Wk),
        "f_a": turned(np.asarray(L0_ffn_A).reshape(ER, D)),
        "f_bm": np.asarray(L0_ffn_Bm).transpose(0, 2, 1).reshape(ER, D),
    }
    nc = bacc.Bacc("TRN2", target_bir_lowering=False, num_devices=1)
    arrays, args = {}, []
    for name, a in laid.items():
        a = np.ascontiguousarray(a)
        arrays[name] = a
        args.append(nc.dram_tensor(name, a.shape, mybir.dt.from_np(a.dtype), kind="ExternalInput").ap())
    result = nc.dram_tensor("out", (B, P, D), F32, kind="ExternalOutput").ap()
    build(nc, *args, result)
    r = run_bass_kernel_spmd(nc, [arrays], core_ids=[0])
    return r.results[0]["out"]
```
